# Optimizing a Trainium2 kernel written in Bass

```python
import numpy as np
import jax
import jax.numpy as jnp

def _softmax(x, axis=-1):
    return jax.nn.softmax(x, axis=axis)

def _gelu(x):
    return jax.nn.gelu(x, approximate=True)

def _silu(x):
    return jax.nn.silu(x)

def _sigmoid(x):
    return jax.nn.sigmoid(x)

def _layernorm(x, axis=-1, eps=1e-05):
    m = jnp.mean(x, axis=axis, keepdims=True)
    v = jnp.var(x, axis=axis, keepdims=True)
    return (x - m) / jnp.sqrt(v + eps)

def _scatter_add(tgt, idx, src, axis=0):
    return tgt.at[idx].add(src)

def _segment_sum(src, seg, n):
    return jax.ops.segment_sum(src, seg, n)
kernel_name = 'mk_decoder_postln_d1_seqx_r8_e1b203'

def setup_inputs(seed: int=0):
    np.random.seed(seed)
    _w = jnp.asarray

    def _rec_inputs():
        import jax
        import jax.numpy as jnp
        _rk = jax.random.key(seed)
        x = -0.0002928 + 1 * jax.random.normal(jax.random.fold_in(_rk, 1), (1, 1024, 128), jnp.float32)
        _lenS = 1024 - jax.random.randint(jax.random.fold_in(_rk, 7), (1,), 0, max(1, 1024 // 4) + 1, jnp.int32)
        _lenS2 = 6404 - jax.random.randint(jax.random.fold_in(_rk, 8), (1,), 0, max(1, 6404 // 4) + 1, jnp.int32)
        _ctx_1024P = jax.random.normal(jax.random.fold_in(_rk, 11), (1, 16, 128), jnp.float32)
        _ctx_1024c = jax.random.dirichlet(jax.random.fold_in(_rk, 511), 0.3 * jnp.ones((16,), jnp.float32), (1, 6404))
        _ctx_1024t = jnp.einsum('bsk,bkd->bsd', _ctx_1024c, _ctx_1024P)
        _ctx_1024t = _ctx_1024t * jax.lax.rsqrt(jnp.mean(jnp.square(_ctx_1024t)) + 1e-12) * 0.953939
        ctx_1024 = -1.39393e-06 + 0.999914 * (_ctx_1024t + 0.3 * jax.random.normal(jax.random.fold_in(_rk, 611), (1, 6404, 128), jnp.float32))
        _validS = jnp.arange(1024)[None, :] < _lenS[:, None]
        _validS2 = jnp.arange(6404)[None, :] < _lenS2[:, None]
        _causal = jnp.tril(jnp.ones((1024, 1024), dtype=bool))
        mask_SxS2_ik0 = jnp.where(jnp.broadcast_to(_validS2[0:1, :], (1024, 6404)), 0, 1).astype(jnp.int32)
        return (x, ctx_1024, mask_SxS2_ik0)
    x, ctx_1024, mask_SxS2_ik0 = _rec_inputs()

    def _L0_attn_setup():
        import jax, jax.numpy as jnp
        import numpy as np
        EMBD = 128
        HEADS = 16
        HEAD_DIM = EMBD // HEADS
        key = jax.random.key(seed)
        ks = jax.random.split(key, 9)
        B, S = (4, 256)
        s = 1.0 / np.sqrt(EMBD)
        return {'x': jax.random.normal(ks[0], (B, S, EMBD), dtype=jnp.float32), 'Wq': jax.random.normal(ks[1], (EMBD, EMBD), dtype=jnp.float32) * s, 'bq': jnp.zeros((EMBD,), dtype=jnp.float32), 'Wk': jax.random.normal(ks[2], (EMBD, HEAD_DIM), dtype=jnp.float32) * s, 'bk': jnp.zeros((HEAD_DIM,), dtype=jnp.float32), 'Wv': jax.random.normal(ks[3], (EMBD, HEAD_DIM), dtype=jnp.float32) * s, 'bv': jnp.zeros((HEAD_DIM,), dtype=jnp.float32), 'Wo': jax.random.normal(ks[4], (EMBD, EMBD), dtype=jnp.float32) * s, 'bo': jnp.zeros((EMBD,), dtype=jnp.float32)}
    _L0_attn_all = _L0_attn_setup()
    _L0_attn_in = {k: v for k, v in _L0_attn_all.items() if k in ('Wq', 'bq', 'Wk', 'bk', 'Wv', 'bv', 'Wo', 'bo')}
    del _L0_attn_all

    def _L0_xattn_setup():
        import jax, jax.numpy as jnp
        import numpy as np
        D_MODEL = 128
        NUM_HEADS = 16
        D_K = D_MODEL // NUM_HEADS
        B, S = (2, 256)
        NEG = -1000000000.0
        key = jax.random.key(seed)
        ks = jax.random.split(key, 12)
        sc = 1.0 / np.sqrt(D_MODEL)
        inp = {'query': jax.random.normal(ks[0], (B, S, D_MODEL), jnp.float32), 'key': jax.random.normal(ks[1], (B, S, D_MODEL), jnp.float32), 'value': jax.random.normal(ks[2], (B, S, D_MODEL), jnp.float32), 'mask': jnp.tril(jnp.ones((S, S), jnp.int32)), 'Wq': jax.random.normal(ks[3], (D_MODEL, D_MODEL), jnp.float32) * sc, 'bq': jnp.zeros((D_MODEL,), jnp.float32), 'Wk': jax.random.normal(ks[4], (D_MODEL, D_MODEL), jnp.float32) * sc, 'bk': jnp.zeros((D_MODEL,), jnp.float32), 'Wv': jax.random.normal(ks[5], (D_MODEL, D_MODEL), jnp.float32) * sc, 'bv': jnp.zeros((D_MODEL,), jnp.float32), 'Wo': jax.random.normal(ks[6], (D_MODEL, D_MODEL), jnp.float32) * sc, 'bo': jnp.zeros((D_MODEL,), jnp.float32)}
        return inp
    _L0_xattn_all = _L0_xattn_setup()
    _L0_xattn_in = {k: v for k, v in _L0_xattn_all.items() if k in ('Wq', 'bq', 'Wk', 'bk', 'Wv', 'bv', 'Wo', 'bo')}
    del _L0_xattn_all

    def _L0_ffn_setup():
        import jax, jax.numpy as jnp
        import numpy as np
        B, S, D, E = (2, 256, 128, 8)
        key = jax.random.key(seed)
        ks = jax.random.split(key, 5)
        x = jax.random.normal(ks[0], (B, S, D), dtype=jnp.float32)
        router_w = jax.random.normal(ks[1], (E, D), dtype=jnp.float32) * 0.02
        router_b = jnp.zeros((E,), dtype=jnp.float32)
        expert_w = jax.random.normal(ks[2], (E, D, D), dtype=jnp.float32) * 0.02
        expert_b = jnp.zeros((E, D), dtype=jnp.float32)
        return {'x': x, 'router_w': router_w, 'router_b': router_b, 'expert_w': expert_w, 'expert_b': expert_b}
    _L0_ffn_all = _L0_ffn_setup()
    _L0_ffn_in = {k: v for k, v in _L0_ffn_all.items() if k in ('router_w', 'router_b', 'expert_w', 'expert_b')}
    del _L0_ffn_all
    return {'x': x, 'ctx_1024': ctx_1024, 'mask_SxS2_ik0': mask_SxS2_ik0, 'L0_attn_Wq': _L0_attn_in['Wq'], 'L0_attn_bq': _L0_attn_in['bq'], 'L0_attn_Wk': _L0_attn_in['Wk'], 'L0_attn_bk': _L0_attn_in['bk'], 'L0_attn_Wv': _L0_attn_in['Wv'], 'L0_attn_bv': _L0_attn_in['bv'], 'L0_attn_Wo': _L0_attn_in['Wo'], 'L0_attn_bo': _L0_attn_in['bo'], 'L0_xattn_Wq': _L0_xattn_in['Wq'], 'L0_xattn_bq': _L0_xattn_in['bq'], 'L0_xattn_Wk': _L0_xattn_in['Wk'], 'L0_xattn_bk': _L0_xattn_in['bk'], 'L0_xattn_Wv': _L0_xattn_in['Wv'], 'L0_xattn_bv': _L0_xattn_in['bv'], 'L0_xattn_Wo': _L0_xattn_in['Wo'], 'L0_xattn_bo': _L0_xattn_in['bo'], 'L0_ffn_router_w': _L0_ffn_in['router_w'], 'L0_ffn_router_b': _L0_ffn_in['router_b'], 'L0_ffn_expert_w': _L0_ffn_in['expert_w'], 'L0_ffn_expert_b': _L0_ffn_in['expert_b']}

def reference(x, ctx_1024, mask_SxS2_ik0, L0_attn_Wq, L0_attn_bq, L0_attn_Wk, L0_attn_bk, L0_attn_Wv, L0_attn_bv, L0_attn_Wo, L0_attn_bo, L0_xattn_Wq, L0_xattn_bq, L0_xattn_Wk, L0_xattn_bk, L0_xattn_Wv, L0_xattn_bv, L0_xattn_Wo, L0_xattn_bo, L0_ffn_router_w, L0_ffn_router_b, L0_ffn_expert_w, L0_ffn_expert_b):
    import jax
    import jax.numpy as jnp

    def _L0_attn_ref(x, Wq, bq, Wk, bk, Wv, bv, Wo, bo):
        import jax, jax.numpy as jnp
        import numpy as np
        EMBD = 128
        HEADS = 16
        HEAD_DIM = EMBD // HEADS
        B, S, _ = x.shape
        Q = (x @ Wq + bq).reshape(B, S, HEADS, HEAD_DIM).transpose(0, 2, 1, 3)
        K = x @ Wk + bk
        V = x @ Wv + bv
        scale = 1.0 / jnp.sqrt(jnp.asarray(HEAD_DIM, dtype=x.dtype))
        scores = jnp.einsum('bhsd,btd->bhst', Q, K) * scale
        attn = jax.nn.softmax(scores, axis=-1)
        out = jnp.einsum('bhst,btd->bhsd', attn, V)
        out = out.transpose(0, 2, 1, 3).reshape(B, S, EMBD)
        return out @ Wo + bo

    def _L0_xattn_ref(query, key, value, mask, Wq, bq, Wk, bk, Wv, bv, Wo, bo):
        import jax, jax.numpy as jnp
        import numpy as np
        D_MODEL = 128
        NUM_HEADS = 16
        D_K = D_MODEL // NUM_HEADS
        B, S = (2, 256)
        NEG = -1000000000.0
        b, s, _ = query.shape
        Q = query @ Wq.T + bq
        K = key @ Wk.T + bk
        V = value @ Wv.T + bv
        Q = Q.reshape(b, s, NUM_HEADS, D_K).transpose(0, 2, 1, 3)
        K = K.reshape(b, -1, NUM_HEADS, D_K).transpose(0, 2, 1, 3)
        V = V.reshape(b, -1, NUM_HEADS, D_K).transpose(0, 2, 1, 3)
        scores = jnp.einsum('bhqd,bhkd->bhqk', Q, K) / np.sqrt(D_K).astype(np.float32)
        scores = jnp.where(mask[None, None, :, :] == 0, NEG, scores)
        attn = jax.nn.softmax(scores, axis=-1)
        out = jnp.einsum('bhqk,bhkd->bhqd', attn, V)
        out = out.transpose(0, 2, 1, 3).reshape(b, s, D_MODEL)
        return out @ Wo.T + bo

    def _L0_ffn_ref(x, router_w, router_b, expert_w, expert_b):
        import jax, jax.numpy as jnp
        import numpy as np
        B, S, D, E = (2, 256, 128, 8)
        logits = jnp.einsum('bsd,ed->bse', x, router_w) + router_b
        probs = jax.nn.softmax(logits, axis=-1)
        weights = jnp.max(probs, axis=-1)
        top1 = jnp.argmax(probs, axis=-1)
        y_all = jnp.einsum('bsd,eod->bseo', x, expert_w) + expert_b
        y = jnp.take_along_axis(y_all, top1[:, :, None, None], axis=2)[:, :, 0, :]
        out = y * weights[:, :, None]
        return out
    x = _layernorm(x + _L0_attn_ref(x, L0_attn_Wq, L0_attn_bq, L0_attn_Wk, L0_attn_bk, L0_attn_Wv, L0_attn_bv, L0_attn_Wo, L0_attn_bo), axis=-1)
    x = _layernorm(x + _L0_xattn_ref(x, ctx_1024, ctx_1024, mask_SxS2_ik0, L0_xattn_Wq, L0_xattn_bq, L0_xattn_Wk, L0_xattn_bk, L0_xattn_Wv, L0_xattn_bv, L0_xattn_Wo, L0_xattn_bo), axis=-1)
    x = _layernorm(x + _L0_ffn_ref(x, L0_ffn_router_w, L0_ffn_router_b, L0_ffn_expert_w, L0_ffn_expert_b), axis=-1)
    return x

_drawn_inputs = setup_inputs


def setup_inputs(seed=0):
    import zlib

    import numpy as np

    out = dict(_drawn_inputs(seed))
    spreads = {'L0_attn_bq': (0.0, 0.8),
     'L0_attn_bk': (0.0, 0.8),
     'L0_attn_bv': (0.0, 0.1),
     'L0_attn_bo': (0.0, 0.1),
     'L0_xattn_bq': (0.0, 0.351),
     'L0_xattn_bk': (0.0, 0.8),
     'L0_xattn_bv': (0.0, 0.1),
     'L0_xattn_bo': (0.0, 0.1),
     'L0_ffn_router_b': (0.0, 0.281),
     'L0_ffn_expert_b': (0.0, 0.442)}
    factors = {}
    for name, (base, spread) in spreads.items():
        noise = np.random.default_rng([zlib.crc32(name.encode()), seed]).standard_normal(out[name].shape)
        drawn = base * np.exp(spread * noise) if base else spread * noise
        out[name] = jnp.asarray(drawn.astype(out[name].dtype))
    for name, factor in factors.items():
        out[name] = (out[name] * factor).astype(out[name].dtype)
    return out
```

```python
from contextlib import ExitStack
from functools import partial

import concourse.bass as bass
from concourse import mybir

F32 = mybir.dt.float32
BF16 = mybir.dt.bfloat16
I32 = mybir.dt.int32
U8 = mybir.dt.uint8
ALU = mybir.AluOpType
ACT = mybir.ActivationFunctionType
AX = mybir.AxisListType
ds = bass.ds

P = 128
D = 128
Q = 1024
QT = Q // P
HEADS = 16
DH = D // HEADS
GH = 2
NG = HEADS // GH
KEYS = 6404
PAIR = 256
NP = -(-KEYS // PAIR)
KPAD = NP * PAIR
FRONT = KPAD - KEYS
NB = KPAD // P
SELF_PAIRS = Q // PAIR
MIN_PAIRS = 3
SPLIT = 3
SROWS = SPLIT * SPLIT * DH
PEN = SROWS
MAXROW = SROWS + 1
KR = MAXROW + SPLIT
CH = GH * PAIR // P
NBANK = GH * QT * PAIR // 512
E = 8
EPS = 1e-5
SCALE = float(DH) ** -0.5
PENALTY = -(2.0 ** 100)
VW = DH + 1


def decoder_layer(nc, t, out):
    ctx = ExitStack()
    with ctx:
        def sb(name, shape, dt=F32):
            return ctx.enter_context(nc.sbuf_tensor(name, shape, dt))

        def ps(name, shape):
            return ctx.enter_context(nc.psum_tensor(name, shape, F32))

        def sem(name):
            return ctx.enter_context(nc.semaphore(name))

        def dram(name, shape, dt):
            return nc.dram_tensor(name, shape, dt, kind="Internal").ap()

        x = sb("x", [P, QT, D])
        xT = sb("xT", [P, Q])
        wq_s, wo_s = sb("wq_s", [P, D]), sb("wo_s", [P, D])
        wq_x, wk_x, wv_x, wo_x = (sb(n, [P, D]) for n in ("wq_x", "wk_x", "wv_x", "wo_x"))
        wk_s, wv_s = sb("wk_s", [P, DH]), sb("wv_s", [P, DH])
        bq_s, bq_x, bk_x = sb("bq_s", [P, 1]), sb("bq_x", [P, 1]), sb("bk_x", [P, 1])
        bk_s = sb("bk_s", [DH, 1])
        bv_s = sb("bv_s", [P, DH])
        bv_x = sb("bv_x", [P, D])
        bo = sb("bo", [P, D])
        ident = sb("ident", [P, P])
        penI = sb("penI", [P, P], BF16)
        ones = sb("ones", [P, P], BF16)
        zrow = sb("zrow", [P, 512], BF16)
        Qs = sb("Qs", [P, HEADS, Q], BF16)
        Kself = sb("Kself", [P, Q], BF16)
        Kx = sb("Kx", [P, 3, GH, KPAD], BF16)
        prob = sb("prob", [P, CH, Q])
        Vs = sb("Vs", [P, Q // P, VW])
        Vx = sb("Vx", [P, NB, HEADS, VW])
        vst = sb("vst", [P, 2, GH, VW])
        real = sb("real", [P, NB])
        ctxs = sb("ctxs", [P, PAIR])
        kf = sb("kf", [P, PAIR])
        kr = sb("kr", [P, PAIR])
        vf = sb("vf", [P, 2, D])
        kp = sb("kp", [P, SPLIT, PAIR], BF16)
        gint = sb("gint", [P, QT, PAIR], I32)
        grow = sb("grow", [P, QT, PAIR], BF16)
        gcol = sb("gcol", [P, QT, PAIR], BF16)
        mx = sb("mx", [P, 2, GH * QT])
        mxt = sb("mxt", [P, GH * QT])
        negm = sb("negm", [GH * QT, P])
        negr = sb("negr", [GH * QT, P])
        mxp = sb("mxp", [GH * QT, SPLIT, P], BF16)
        osb = sb("osb", [P, 512])
        rden = sb("rden", [P, 4, 2 * GH])
        attn = sb("attn", [P, QT, D])
        cnt = sb("cnt", [P, NB])
        lp = sb("lp", [P, 2 * NB], BF16)
        sm = sb("sm", [P, 2, NP])
        down = sb("down", [P, NP])
        steer = sb("steer", [1, 4], I32)
        sc1 = sb("sc1", [P, 8])
        penr = sb("penr", [NB, P], BF16)
        stat = sb("stat", [P, QT, 6])
        mv = sb("mv", [P, QT, 2])
        rstd = sb("rstd", [P, QT])
        eps = sb("eps", [P, 1])
        lg = sb("lg", [P, 6, QT, E])
        rsm = sb("rsm", [P, 4, QT])
        wr = sb("wr", [P, E])
        br = sb("br", [P, E])
        be = sb("be", [E, D])
        coefT = sb("coefT", [E, P])

        qf, qr = prob[:, 0, :], prob[:, 1, :]
        qp = prob[:, 2:4, :].bitcast(BF16)[:, :, :].rearrange("p a q -> p (a q)")[:, 0:SPLIT * Q] \
            .rearrange("p (a q) -> p a q", a=SPLIT)
        aT = prob[:, 0, :]
        kp8 = [m_[0:DH, h * 4:h * 4 + 4, :].rearrange("p a b -> p (a b)") for m_, h in ((grow, 0), (grow, 1), (gcol, 0))]
        kf8 = gint[0:DH, 0:4, :].rearrange("p a b -> p (a b)").bitcast(F32)
        kr8 = gint[0:DH, 4:8, :].rearrange("p a b -> p (a b)").bitcast(F32)
        maskI = [Kx[:, b, :, :].rearrange("p h k -> p (h k)").bitcast(I32) for b in range(2)]
        dead8 = Kx[:, 2, 0, 0:KPAD // 2].bitcast(U8)
        acc8 = Kx[:, 2, 0, KPAD // 2:KPAD].bitcast(U8)
        acc = Kx[:, 2, 1, :]
        we = Kx[:, 0, :, :].rearrange("p h k -> p (h k)")[:, 0:2 * E * D].bitcast(F32) \
            .rearrange("p (e o) -> p e o", e=E)

        qd = dram("qd", [SPLIT, D, Q], BF16)
        ksd = dram("ksd", [SPLIT * DH, Q], BF16)
        kd = dram("kd", [HEADS, SPLIT * DH, KPAD], BF16)
        tail = dram("tail", [1 + SPLIT, KPAD], BF16)

        ST = [ps(f"ST{n}", [P, Q]) for n in range(2)]
        SR_BANK = (0, 1, 2, 0, 1, 2, 0, 1)
        SR_BACK = (2, 2, 4, 3, 3, 3, 3, 3)
        SR = [ps(f"SR{n}", [P, 512]) for n in range(2)]
        O = ps("O", [P, 512])
        M = ps("M", [P, 512])
        SR.append(M)

        sems = {n_: sem(n_) for n_ in (
            "in_x in_w cst0 cst q_out k_out k_in krow s_k_ready s_k_ev s_k_parts s_v_ready vs_ones vs_made "
            "mask_in0 mask_in1 mask_used mask_added mask_counts counted flags flag_sums steered pen_made "
            "ctx_in x_k_ready x_k_ev x_k_parts kd_out x_v_ready vf_made vx_made kx_in0 kx_in1 kx_in2 "
            "v_staged grow_in grow_ready grow_free gcol_in gcol_ready gcol_free dve_chain "
            "passed bo2 logits shifted router_exp coef coefT coefT_copied y_all y_bias f_res f_var f_std "
            "out_done stored").split()}
        for a_ in "sx":
            for n_ in ("q_ready q_parts q_in row_ready row_free mx mx_turned mx_copied mx_chain mx_parts "
                       "max_in0 max_in1 col_ready exp pv o_copied o_turned rden normed aT aT_copied y res "
                       "var std x xT xT_copied").split():
                sems[f"{a_}_{n_}"] = sem(f"{a_}_{n_}")

        def S(name):
            return sems[name]

        block = ctx.enter_context(nc.Block())

        def kstack(a, g, rows, hh, start, size):
            if a == "s":
                return Kself[0:rows, ds(start, size)]
            return Kx[0:rows, g % 3, hh, ds(start, size)]

        def loop(eng, start, end):
            if isinstance(end, int):
                yield from range(start, end)
            else:
                with eng.Fori(start, end) as i:
                    yield i

        def at(eng, value):
            return value if isinstance(value, int) else eng.snap(value)

        def wait_count(eng, semaphore, value):
            eng.wait_ge(semaphore, value)
            eng.sem_inc(S("passed"), 1)

        def pe_attention(pe, a, n, n1, general):
            rows_r = SROWS if a == "s" else SROWS + 1

            def row_bank(g, U, i, j):
                pe.wait_ge(S(a + "_row_free"), U * NBANK + (j + 3 - SR_BACK[j]))
                hh = j // (NBANK // GH)
                for r in range(2):
                    qt = 2 * (j % (NBANK // GH)) + r
                    o = SR[SR_BANK[j]][:, r * PAIR:(r + 1) * PAIR]
                    mm = nc.tensor.matmul(o, Qs[0:rows_r, GH * g + hh, qt * P:(qt + 1) * P],
                                          kstack(a, g, rows_r, hh, i * PAIR, PAIR),
                                          start=True, stop=not general, skip_group_check=True)
                    if general:
                        mm = nc.tensor.matmul(o, penI[:, :], grow[:, qt, :], start=False, stop=True,
                                              skip_group_check=True)
                mm.then_inc(S(a + "_row_ready"), 1)

            def row_begin(U):
                if general:
                    pe.wait_ge(S("grow_ready"), U + 1)

            def row_end():
                if general:
                    pe.drain().then_inc(S("grow_free"), 1)

            def column(g, T, i, c):
                b, hh = c // GH, c % GH
                pe.wait_ge(S(a + "_exp"), T * CH + (c + 1))
                if general and c == 0:
                    pe.wait_ge(S("gcol_ready"), T + 1)
                for half in range(2):
                    mm = nc.tensor.matmul(ST[c % 2][:, half * 512:(half + 1) * 512],
                                          kstack(a, g, KR, hh, i * PAIR + b * P, P),
                                          Qs[0:KR, GH * g + hh, half * 512:(half + 1) * 512],
                                          start=True, stop=not general, skip_group_check=True)
                    if general:
                        for qt in range(4 * half, 4 * half + 4):
                            mm = nc.tensor.matmul(ST[c % 2][:, qt * P:(qt + 1) * P],
                                                  gcol[:, qt, b * P:(b + 1) * P], penI[:, :],
                                                  start=False, stop=(qt % 4 == 3),
                                                  skip_group_check=True)
                mm.then_inc(S(a + "_col_ready"), 1)
                if general and c == CH - 1:
                    pe.drain().then_inc(S("gcol_free"), 1)

            def values(T, i, b, back=0):
                pe.wait_ge(S(a + "_exp"), T * CH + (GH * b + GH + 2 - CH * back))
                if a == "x":
                    pe.wait_ge(S("v_staged"), T * 2 + (b + 1 - 2 * back))
                for hh in range(GH):
                    for half in range(2):
                        r = 32 * (2 * hh + half)
                        v = Vs[:, 2 * i + b, :] if a == "s" else vst[:, b, hh, :]
                        mm = nc.tensor.matmul(O[r:r + VW, :], v,
                                              prob[:, GH * b + hh, half * 512:(half + 1) * 512],
                                              start=False, stop=False, skip_group_check=True)
                mm.then_inc(S(a + "_pv"), 1)

            def clear_o(g):
                if g:
                    pe.wait_ge(S(a + "_o_copied"), g)
                nc.tensor.matmul(O[:, :], zrow[:, 0:P], zrow[:, :], start=True, stop=False,
                                 skip_group_check=True)

            def max_turn(g):
                pe.wait_ge(S(a + "_mx"), n1 * (g + 1))
                if g:
                    pe.wait_ge(S(a + "_mx_copied"), g)
                if g >= 2:
                    pe.wait_ge(S(a + "_normed"), g - 1)
                nc.tensor.transpose(M[0:GH * QT, 0:P], mx[:, g % 2, :], ident[:, :]) \
                    .then_inc(S(a + "_mx_turned"), 1)

            def o_turn(g):
                pe.wait_ge(S(a + "_o_copied"), g + 1)
                pe.wait_ge(S(a + "_mx_copied"), min(g + 2, NG))
                if g:
                    pe.wait_ge(S(a + "_normed"), g)
                for t_ in range(4):
                    mm = nc.tensor.transpose(M[:, t_ * P:(t_ + 1) * P], osb[:, t_ * P:(t_ + 1) * P],
                                             ident[:, :])
                mm.then_inc(S(a + "_o_turned"), 1)

            def loaded(g):
                if a == "x":
                    pe.wait_ge(S(f"kx_in{g % 3}"), n * (4 * 16 * (g // 3 + 1)))

            loaded(0)
            row_begin(0)
            for j in range(NBANK):
                row_bank(0, 0, 0, j)
            row_end()
            for i in loop(pe, 1, n):
                row_begin(i)
                for j in range(NBANK):
                    row_bank(0, i, i, j)
                row_end()
            loaded(1)
            row_begin(n)
            for j in range(NBANK):
                if j == 2:
                    max_turn(0)
                    pe.wait_ge(S(a + "_mx_copied"), 1)
                row_bank(1, n, 0, j)
            row_end()

            def step(g, T, i, rg, ri, first=False, last=False):
                U = at(pe, T + n + 1) if rg < NG else None

                def rows(j):
                    if rg < NG:
                        row_bank(rg, U, ri, j)

                def before():
                    if not (first and g == 0):
                        values(T, (i - 1) % n if a == "s" else None, 1, back=1)

                if rg < NG:
                    row_begin(U)
                rows(0)
                if first:
                    rows(1), before(), rows(2)
                    pe.wait_ge(S(f"{a}_max_in{g % 2}"), 16 * SPLIT * (g // 2 + 1))
                    column(g, T, i, 0), rows(3), column(g, T, i, 1)
                else:
                    column(g, T, i, 0), rows(1)
                    if last and g + 1 < NG:
                        max_turn(g + 1)
                    before()
                    if last and g + 1 < NG:
                        pe.wait_ge(S(a + "_mx_copied"), g + 2)
                    elif g:
                        pe.wait_ge(S(a + "_normed"), g)
                    rows(2), column(g, T, i, 1), rows(3)
                rows(4), column(g, T, i, 2), rows(5)
                if first:
                    clear_o(g)
                values(T, i, 0), rows(6), column(g, T, i, 3), rows(7)
                if rg < NG:
                    row_end()
                if first and g:
                    if rg < NG:
                        pe.wait_ge(S(a + "_row_free"), U * NBANK + NBANK)
                    o_turn(g - 1)

            for g in range(NG):
                T0 = at(pe, n * g)
                step(g, T0, 0, g + 1, 1, first=True)
                for i in loop(pe, 1, n1):
                    step(g, at(pe, T0 + i), i, g + 1, i + 1)
                if g + 2 < NG:
                    loaded(g + 2)
                step(g, at(pe, T0 + n1), n1, g + 2, 0, last=True)
            values(at(pe, n * NG), n1 if a == "s" else None, 1, back=1)
            o_turn(NG - 1)

        def act_attention(act, a, n):
            def step(T):
                for c in range(CH):
                    act.wait_ge(S(a + "_col_ready"), T * CH + (c + 1))
                    if c % GH == 0:
                        act.wait_ge(S(a + "_pv"), T * 2 + (c // GH + 1))
                    nc.scalar.activation(prob[:, c, :], ST[c % 2][:, :], ACT.Exp).then_inc(S(a + "_exp"), 1)

            def copy_o(g):
                act.wait_ge(S(a + "_pv"), n * (2 * (g + 1)) + 2)
                if g:
                    act.wait_ge(S(a + "_o_turned"), g)
                nc.scalar.copy(osb[:, :], O[:, :]).then_inc(S(a + "_o_copied"), 1)

            for g in range(NG):
                T0 = at(act, n * g)
                if g:
                    copy_o(g - 1)
                step(T0)
                with act.Fori(1, n) as i:
                    step(at(act, T0 + i))
            copy_o(NG - 1)

        def dve_attention(dve, a, n, n1):
            parts = [0]

            def row_max(g, U, j, first):
                dve.wait_ge(S(a + "_row_ready"), U * NBANK + (j + 1))
                o = mx[:, g % 2, 2 * j:2 * j + 2] if first else mxt[:, 2 * j:2 * j + 2]
                nc.vector.tensor_reduce(o, SR[SR_BANK[j]][:, :].rearrange("p (r k) -> p r k", r=2), AX.X,
                                        ALU.max).then_inc(S(a + "_row_free"), 1)

            def row_later(g, U, updates):
                for j in range(NBANK):
                    row_max(g, U, j, False)
                dve.wait_ge(S(a + "_row_free"), U * NBANK + (NBANK + 2))
                nc.vector.tensor_tensor(mx[:, g % 2, :], mx[:, g % 2, :], mxt[:, :], ALU.max) \
                    .then_inc(S(a + "_mx"), 1)
                (dve.wait_ge if a == "s" else partial(wait_count, dve))(S(a + "_mx"), updates)

            def split_max(g):
                def chain(ins):
                    parts[0] += 1
                    ins.then_inc(S(a + "_mx_chain"), 1)
                    dve.wait_ge(S(a + "_mx_chain"), parts[0])

                dve.wait_ge(S(a + "_mx_turned"), g + 1)
                if g:
                    dve.wait_ge(S(f"{a}_max_in{(g - 1) % 2}"), 16 * SPLIT * ((g - 1) // 2 + 1))
                nc.vector.tensor_scalar(negm[:, :], M[0:GH * QT, 0:P], -1.0, None, ALU.mult) \
                    .then_inc(S(a + "_mx_copied"), 1)
                dve.wait_ge(S(a + "_mx_copied"), g + 1)
                chain(nc.vector.tensor_copy(mxp[:, 0, :], negm[:, :]))
                chain(nc.vector.tensor_tensor(negr[:, :], negm[:, :], mxp[:, 0, :], ALU.subtract))
                chain(nc.vector.tensor_copy(mxp[:, 1, :], negr[:, :]))
                chain(nc.vector.tensor_tensor(negm[:, :], negr[:, :], mxp[:, 1, :], ALU.subtract))
                nc.vector.tensor_copy(mxp[:, 2, :], negm[:, :]).then_inc(S(a + "_mx_parts"), 1)
                dve.wait_ge(S(a + "_mx_parts"), g + 1)

            def normalise(g):
                dve.wait_ge(S(a + "_o_turned"), g + 1)
                o = M[:, :].rearrange("p (t h f r) -> p t h f r", t=4, h=GH, f=2)
                nc.vector.reciprocal(rden[:, :, :], M[:, :].rearrange("p (t s r) -> p t s r", t=4, s=4)
                                     [:, :, :, DH]).then_inc(S(a + "_rden"), 1)
                dve.wait_ge(S(a + "_rden"), g + 1)
                rd = rden[:, :, :].rearrange("p t (h f) -> p t h f", h=GH)
                for hh in range(GH):
                    for half in range(2):
                        h0 = (GH * g + hh) * DH
                        ins = nc.vector.tensor_tensor(
                            attn[:, 4 * half:4 * half + 4, h0:h0 + DH], o[:, :, hh, half, 0:DH],
                            rd[:, :, hh, half].unsqueeze(2).to_broadcast([P, 4, DH]), ALU.mult)
                ins.then_inc(S(a + "_normed"), 1)

            dve.sem_inc(S(a + "_row_free"), 2)
            for j in range(NBANK):
                row_max(0, 0, j, True)
            for i in loop(dve, 1, n):
                row_later(0, i, i)
            for j in range(NBANK):
                row_max(1, n, j, True)
                if j == 1:
                    split_max(0)
            for g in range(NG):
                T0 = at(dve, n * g)
                done = at(dve, n1 * (g + 1))
                if g + 1 < NG:
                    row_later(g + 1, at(dve, T0 + n + 1), done + 1)
                if g:
                    normalise(g - 1)
                if g + 1 < NG:
                    for i in loop(dve, 1, n1):
                        row_later(g + 1, at(dve, T0 + n + 1 + i), done + 1 + i)
                    U = at(dve, T0 + n + n)
                    for j in range(NBANK):
                        if g + 2 < NG:
                            row_max(g + 2, U, j, True)
                        if j == 1:
                            split_max(g + 1)
            normalise(NG - 1)

        def sp_max_rows(sp, a, g):
            sp.wait_ge(S(a + "_mx_parts"), g + 1)
            for k in range(SPLIT):
                sp.dma_start(Qs[MAXROW + k:MAXROW + k + 1, GH * g:GH * (g + 1), :]
                             .rearrange("o h (t f) -> o (h t) f", f=P),
                             mxp[:, k, :]).then_inc(S(f"{a}_max_in{g % 2}"), 16)

        def split3(e, src, rest, parts, chain):
            chain(e.tensor_copy(parts[0], src))
            chain(e.tensor_tensor(rest, src, parts[0], ALU.subtract))
            chain(e.tensor_copy(parts[1], rest))
            chain(e.tensor_tensor(src, rest, parts[1], ALU.subtract))
            chain(e.tensor_copy(parts[2], src))

        def chainer(eng, name):
            n_ = [0]

            def chain(ins):
                n_[0] += 1
                ins.then_inc(S(name), 1)
                eng.wait_ge(S(name), n_[0])
            return chain

        @block.sync
        def _(sp):
            def load(dst, src, name):
                sp.dma_start(dst, src).then_inc(S(name), 16)

            load(xT[:, :], t["xT"], "in_x")
            load(wq_s[:, :], t["wq_s"], "in_x")
            load(wk_s[:, :], t["wk_s"], "in_x")
            load(wv_s[:, :], t["wv_s"], "in_x")
            load(bq_s[:, :], t["bq_s"].rearrange("(p o) -> p o", o=1), "in_x")
            load(bk_s[:, :], t["bk_s"].rearrange("(p o) -> p o", o=1), "in_x")
            load(bv_s[:, :], t["bv_s"].rearrange("(o f) -> o f", o=1).to_broadcast([P, DH]), "in_x")
            load(x[:, :, :], t["x"].rearrange("(t p) d -> p t d", p=P), "in_w")
            load(wo_s[:, :], t["wo_s"], "in_w")
            load(bo[:, :], t["bo_s"].rearrange("(o f) -> o f", o=1).to_broadcast([P, D]), "in_w")
            for n_, b_ in (("wq_x", wq_x), ("wk_x", wk_x), ("wv_x", wv_x), ("wo_x", wo_x)):
                load(b_[:, :], t[n_], "in_w")
            load(bq_x[:, :], t["bq_x"].rearrange("(p o) -> p o", o=1), "in_w")
            load(bk_x[:, :], t["bk_x"].rearrange("(p o) -> p o", o=1), "in_w")
            load(bv_x[:, :], t["bv_x"].rearrange("(o f) -> o f", o=1).to_broadcast([P, D]), "in_w")
            load(wr[:, :], t["wr"], "in_w")
            load(br[:, :], t["br"].rearrange("(o f) -> o f", o=1).to_broadcast([P, E]), "in_w")
            load(be[:, :], t["be"], "in_w")
            load(down[:, :], t["countdown"].rearrange("(o f) -> o f", o=1).to_broadcast([P, NP]), "in_w")
            sp.wait_ge(S("cst"), 8)
            for h in range(2):
                load(Kself[PEN:PEN + 1, h * 512:(h + 1) * 512], zrow[0:1, :], "krow")
            for k in range(SPLIT):
                load(tail[1 + k, :].rearrange("(a b) -> a b", a=NB), ones[0:NB, :], "krow")

            def stack_q(a):
                base = {"s": 0, "x": 1}[a]
                for k in range(SPLIT):
                    sp.wait_ge(S(a + "_q_parts"), 2 * k + 1)
                    load(qd[k], qp[:, k, :], "q_out")
                sp.wait_ge(S("q_out"), 48 * (base + 1))
                for k in range(SPLIT):
                    for b in range(SPLIT):
                        r = (k * SPLIT + b) * DH
                        load(Qs[r:r + DH, :, :], qd[k].rearrange("(h d) q -> d h q", d=DH), a + "_q_in")

            sp.wait_ge(S("s_k_parts"), 5)
            for b in range(SPLIT):
                load(ksd[b * DH:(b + 1) * DH, :], kp8[b], "k_out")
            stack_q("s")
            sp.wait_ge(S("k_out"), 48)
            for k in range(SPLIT):
                load(Kself[k * SPLIT * DH:(k + 1) * SPLIT * DH, :], ksd[:, :], "k_in")
            for g in range(NG):
                sp_max_rows(sp, "s", g)

            sp.wait_ge(S("steered"), 1)
            p0 = sp.snap(sp.value_load(steer[0:1, 0:1], min_val=0, max_val=NP - MIN_PAIRS))
            n = sp.snap(sp.value_load(steer[0:1, 1:2], min_val=MIN_PAIRS, max_val=NP))
            sp.wait_ge(S("pen_made"), 1)
            load(tail[0, :].rearrange("(a b) -> a b", a=NB), penr[:, :], "krow")
            with sp.Fori(0, n) as i:
                p = sp.snap(nc.s_assert_within(p0 + i, 0, NP - 1))
                wait_count(sp, S("x_v_ready"), i)
                sp.dma_start(ctxs[:, :], t["ctxT"][:, ds(p * PAIR, PAIR)]).then_inc(S("ctx_in"), 16)
                wait_count(sp, S("x_k_parts"), (i + 1) * 5)
                for b in range(SPLIT):
                    sp.dma_start(kd[:, b * DH:(b + 1) * DH, ds(i * PAIR, PAIR)], kp[:, b, :]) \
                        .then_inc(S("kd_out"), 16)
                wait_count(sp, S("kd_out"), (i + 1) * 48)
            stack_q("x")
            sp.wait_ge(S("krow"), 16 * (2 + SPLIT + 1))

            def load_k(g):
                if g >= 3:
                    wait_count(sp, S("x_pv"), n * (2 * (g - 2)) + 2)
                with sp.Fori(0, n) as i:
                    p = sp.snap(nc.s_assert_within(p0 + i, 0, NP - 1))
                    for k in range(SPLIT):
                        sp.dma_start(Kx[k * SPLIT * DH:(k + 1) * SPLIT * DH, g % 3, :, ds(i * PAIR, PAIR)],
                                     kd[GH * g:GH * (g + 1), :, ds(i * PAIR, PAIR)].rearrange("h r k -> r h k")) \
                            .then_inc(S(f"kx_in{g % 3}"), 16)
                    sp.dma_start(Kx[PEN:KR, g % 3, :, ds(i * PAIR, PAIR)],
                                 tail[:, ds(p * PAIR, PAIR)].rearrange("r (o k) -> r o k", o=1)
                                 .to_broadcast([1 + SPLIT, GH, PAIR])) \
                        .then_inc(S(f"kx_in{g % 3}"), 16)

            sp.wait_ge(S("counted"), 1)
            for g in range(3):
                load_k(g)
            for g in range(NG):
                sp_max_rows(sp, "x", g)
                if g >= 1 and g + 2 < NG:
                    load_k(g + 2)
            sp.wait_ge(S("x_normed"), NG)
            load(bo[:, :], t["bo_x"].rearrange("(o f) -> o f", o=1).to_broadcast([P, D]), "bo2")
            load(we, t["we"].rearrange("d (e o) -> d e o", e=E), "bo2")
            for q in range(QT):
                sp.wait_ge(S("out_done"), q + 1)
                load(out.rearrange("(t p) d -> p t d", p=P)[:, q, :], attn[:, q, :], "stored")
            sp.wait_ge(S("stored"), 16 * QT)

        @block.gpsimd
        def _(pool):
            g_ = nc.gpsimd
            g_.memset(ident[:, :], 0.0).then_inc(S("cst0"), 1)
            g_.memset(penI[:, :], 0.0).then_inc(S("cst0"), 1)
            g_.memset(real[:, :], 1.0).then_inc(S("cst0"), 1)
            pool.wait_ge(S("cst0"), 3)
            g_.affine_select(out=ident[:, :], in_=ident[:, :], compare_op=ALU.not_equal, fill=1.0, base=0,
                             pattern=[[-1, P]], channel_multiplier=1).then_inc(S("cst"), 1)
            g_.affine_select(out=penI[:, :], in_=penI[:, :], compare_op=ALU.not_equal, fill=PENALTY, base=0,
                             pattern=[[-1, P]], channel_multiplier=1).then_inc(S("cst"), 1)
            g_.affine_select(out=real[:, :], in_=real[:, :], compare_op=ALU.is_ge, fill=0.0, base=-FRONT,
                             pattern=[[P, NB]], channel_multiplier=1).then_inc(S("cst"), 1)
            g_.memset(ones[:, :], 1.0).then_inc(S("cst"), 1)
            g_.memset(zrow[:, :], 0.0).then_inc(S("cst"), 1)
            g_.memset(eps[:, :], EPS).then_inc(S("cst"), 1)
            pool.wait_ge(S("s_k_ev"), 1)
            ch = chainer(pool, "s_k_parts")
            split3(g_, kf8, kr8, [kp8[b] for b in range(SPLIT)], ch)
            half = KPAD // 4

            def load_mask(q):
                if q >= 2:
                    pool.wait_ge(S("mask_used"), 4 * (q - 1))
                pool.dma_start(maskI[q % 2], t["mask"][q * P:(q + 1) * P, :]).then_inc(S(f"mask_in{q % 2}"), 16)

            load_mask(0)
            load_mask(1)
            for q in range(QT):
                pool.wait_ge(S(f"mask_in{q % 2}"), 16 * (q // 2 + 1))
                dst = acc8 if q == 0 else dead8
                for c in range(4):
                    w = slice(c * half, (c + 1) * half)
                    g_.tensor_scalar(dst[:, w], maskI[q % 2][:, w], 0.0, None, ALU.is_equal) \
                        .then_inc(S("mask_used"), 1)
                pool.wait_ge(S("mask_used"), 4 * (q + 1))
                if q:
                    g_.tensor_tensor(acc8.bitcast(I32), acc8.bitcast(I32), dead8.bitcast(I32), ALU.add) \
                        .then_inc(S("mask_added"), 1)
                    pool.wait_ge(S("mask_added"), q)
                if q + 2 < QT:
                    load_mask(q + 2)
            g_.tensor_copy(acc[:, :], acc8).then_inc(S("mask_counts"), 1)
            pool.wait_ge(S("steered"), 1)
            n = pool.snap(pool.value_load(steer[0:1, 1:2], min_val=MIN_PAIRS, max_val=NP))
            n1 = pool.snap(pool.value_load(steer[0:1, 3:4], min_val=MIN_PAIRS - 1, max_val=NP - 1))
            general = pool.snap(pool.value_load(steer[0:1, 2:3], min_val=0, max_val=1))
            with pool.Fori(0, n) as i:
                wait_count(pool, S("x_k_ev"), i + 1)
                wait_count(pool, S("kd_out"), i * 48)
                c5 = pool.snap(i * 5)
                k = [0]

                def ch(ins):
                    k[0] += 1
                    ins.then_inc(S("x_k_parts"), 1)
                    wait_count(pool, S("x_k_parts"), c5 + k[0])
                split3(g_, kf[:, :], kr[:, :], [kp[:, b, :] for b in range(SPLIT)], ch)

            def stage_v(g, T, i, b):
                wait_count(pool, S("x_pv"), T * 2 + (b + 1))
                g_.tensor_copy(vst[:, b, :, :], Vx[:, ds(i * 2 + b, 1), GH * g:GH * (g + 1), :]
                               .rearrange("p o h d -> p (o h) d")).then_inc(S("v_staged"), 1)

            def gen_fetch(dst, view, U, i):
                wait_count(pool, S(view + "_free"), U + 1)
                pool.dma_start(gint[:, :, :], t["mask"].rearrange("(t p) k -> p t k", p=P)
                               [:, :, ds(i * PAIR, PAIR)]).then_inc(S(view + "_in"), 16)
                wait_count(pool, S(view + "_in"), U * 16 + 16)
                g_.tensor_scalar(dst[:, :, :], gint[:, :, :], 0.0, None, ALU.is_equal) \
                    .then_inc(S(view + "_ready"), 1)
                wait_count(pool, S(view + "_ready"), U + 1)

            def stream(gen):
                if gen:
                    pool.sem_inc(S("grow_free"), 1)
                    pool.sem_inc(S("gcol_free"), 1)
                    with pool.Fori(0, n) as i:
                        gen_fetch(grow, "grow", i, i)
                    gen_fetch(grow, "grow", n, 0)

                def step(g, T, i, gr, ir):
                    if gen:
                        gen_fetch(gcol, "gcol", T, i)
                        if gr < NG:
                            gen_fetch(grow, "grow", pool.snap(T + n + 1), ir)
                    stage_v(g, T, i, 0)
                    stage_v(g, T, i, 1)

                for g in range(NG):
                    T0 = at(pool, n * g)
                    with pool.Fori(0, n1) as i:
                        step(g, pool.snap(T0 + i), i, g + 1, i + 1)
                    step(g, pool.snap(T0 + n1), n1, g + 2, 0)

            wait_count(pool, S("vx_made"), n * 4)
            with pool.If(general == 1):
                stream(True)
            with pool.Else():
                stream(False)

        def layer_norm(dve, a, chain):
            for q in range(QT):
                dve.wait_ge(S(a + "_res"), q + 1)
                chain(nc.vector.bn_stats(stat[:, q, :], x[:, q, :]))
                nc.vector.bn_aggr(mv[:, q, :], stat[:, q, :]).then_inc(S(a + "_var"), 1)
            dve.wait_ge(S(a + "_std"), 1)
            chain(nc.vector.reciprocal(rstd[:, :], rstd[:, :]))

        @block.vector
        def _(dve):
            v = nc.vector
            ch = chainer(dve, "dve_chain")
            v.memset(Kself[64:96, :], 1.0).then_inc(S("cst"), 1)
            v.memset(Qs[64:96, :, :], 1.0).then_inc(S("cst"), 1)
            v.memset(Vs[:, :, :], 1.0).then_inc(S("vs_ones"), 1)

            def scaled_q(a, bq):
                dve.wait_ge(S(a + "_q_ready"), 1)
                dve.wait_ge(S("in_x" if a == "s" else "in_w"), 16 * (7 if a == "s" else 14))
                ch(v.tensor_scalar(qf, ST[0][:, :], bq[:, 0:1], SCALE, ALU.add, ALU.mult))
                n_ = [0]

                def c2(ins):
                    n_[0] += 1
                    ins.then_inc(S(a + "_q_parts"), 1)
                    dve.wait_ge(S(a + "_q_parts"), n_[0])
                split3(v, qf, qr, [qp[:, b, :] for b in range(SPLIT)], c2)

            dve.wait_ge(S("s_k_ready"), 1)
            v.tensor_scalar(kf8, ST[1][0:DH, :], bk_s[:, 0:1], None, ALU.add).then_inc(S("s_k_ev"), 1)
            scaled_q("s", bq_s)
            dve.wait_ge(S("s_v_ready"), 1)
            dve.wait_ge(S("vs_ones"), 1)
            v.tensor_tensor(Vs[:, :, 0:DH], M[:, 0:QT * DH].rearrange("p (b d) -> p b d", d=DH),
                            bv_s[:, :].unsqueeze(1).to_broadcast([P, QT, DH]), ALU.add) \
                .then_inc(S("vs_made"), 1)

            dve_attention(dve, "s", SELF_PAIRS, SELF_PAIRS - 1)

            def project_out(a):
                dve.wait_ge(S(a + "_aT"), 1)
                v.tensor_copy(aT, ST[0][:, :]).then_inc(S(a + "_aT_copied"), 1)
                dve.wait_ge(S("in_w"), 16 * 14)
                if a == "x":
                    dve.wait_ge(S("bo2"), 32)
                for q in range(QT):
                    dve.wait_ge(S(a + "_y"), q // 4 + 1)
                    ch(v.tensor_tensor(x[:, q, :], x[:, q, :], ST[1][:, q * D:(q + 1) * D], ALU.add))
                    v.tensor_tensor(x[:, q, :], x[:, q, :], bo[:, :], ALU.add).then_inc(S(a + "_res"), 1)
                layer_norm(dve, a, ch)
                for q in range(QT):
                    v.tensor_scalar(x[:, q, :], x[:, q, :], mv[:, q, 0:1], rstd[:, q:q + 1],
                                    ALU.subtract, ALU.mult).then_inc(S(a + "_x"), 1)
                dve.wait_ge(S(a + "_xT"), 1)
                v.tensor_copy(xT[:, :], ST[0][:, :]).then_inc(S(a + "_xT_copied"), 1)

            dve.wait_ge(S("counted"), 1)
            ch(v.tensor_copy(cnt[:, :], M[:, 0:NB]))
            ch(v.tensor_scalar(lp[:, 0:NB], cnt[:, :], float(Q), None, ALU.is_lt))
            v.scalar_tensor_tensor(out=lp[:, NB:2 * NB], in0=cnt[:, :], scalar=0.0, in1=lp[:, 0:NB],
                                   op0=ALU.is_gt, op1=ALU.mult).then_inc(S("flags"), 1)
            dve.wait_ge(S("flag_sums"), 1)
            ch(v.tensor_reduce(sm[:, 0, :], M[:, 64:64 + NB].rearrange("p (k b) -> p k b", b=2), AX.X, ALU.max))
            ch(v.tensor_reduce(sc1[:, 1:2], M[:, 64 + NB:64 + 2 * NB], AX.X, ALU.max))
            ch(v.tensor_scalar(sm[:, 0, :], sm[:, 0, :], 0.0, None, ALU.is_gt))
            dve.wait_ge(S("in_w"), 16 * 14)
            ch(v.tensor_tensor(sm[:, 1, :], sm[:, 0, :], down[:, :], ALU.mult))
            ch(v.tensor_reduce(sc1[:, 2:3], sm[:, 1, :], AX.X, ALU.max))
            ch(v.tensor_scalar(sc1[:, 3:4], sc1[:, 2:3], 0.0, None, ALU.is_equal))
            ch(v.tensor_scalar(sc1[:, 4:5], sc1[:, 1:2], 0.0, None, ALU.is_gt))
            ch(v.tensor_tensor(sc1[:, 5:6], sc1[:, 3:4], sc1[:, 4:5], ALU.max))
            ch(v.tensor_scalar(sc1[:, 6:7], sc1[:, 5:6], float(NP), None, ALU.mult))
            ch(v.tensor_tensor(sc1[:, 6:7], sc1[:, 6:7], sc1[:, 2:3], ALU.max))
            ch(v.tensor_scalar(sc1[:, 6:7], sc1[:, 6:7], float(MIN_PAIRS), None, ALU.max))
            ch(v.tensor_scalar(sc1[:, 7:8], sc1[:, 6:7], -1.0, float(NP), ALU.mult, ALU.add))
            ch(v.tensor_copy(steer[0:1, 0:1], sc1[0:1, 7:8]))
            ch(v.tensor_copy(steer[0:1, 1:2], sc1[0:1, 6:7]))
            ch(v.tensor_scalar(steer[0:1, 3:4], sc1[0:1, 6:7], -1.0, None, ALU.add))
            v.tensor_copy(steer[0:1, 2:3], sc1[0:1, 5:6]).then_inc(S("steered"), 1)
            ch(v.tensor_scalar(sc1[:, 0:1], sc1[:, 5:6], -PENALTY, PENALTY, ALU.mult, ALU.add))
            v.tensor_scalar(penr[:, :], M[0:NB, 192:192 + P], float(Q), sc1[0:NB, 0:1], ALU.is_equal,
                            ALU.mult).then_inc(S("pen_made"), 1)
            dve.wait_ge(S("pen_made"), 1)
            n = dve.snap(dve.value_load(steer[0:1, 1:2], min_val=MIN_PAIRS, max_val=NP))
            n1 = dve.snap(dve.value_load(steer[0:1, 3:4], min_val=MIN_PAIRS - 1, max_val=NP - 1))
            p0 = dve.snap(dve.value_load(steer[0:1, 0:1], min_val=0, max_val=NP - MIN_PAIRS))
            with dve.Fori(0, n) as i:
                dve.wait_ge(S("x_k_ready"), i + 1)
                dve.wait_ge(S("x_k_parts"), i * 5)
                v.tensor_scalar(kf[:, :], ST[0][:, 0:PAIR], bk_x[:, 0:1], None, ALU.add).then_inc(S("x_k_ev"), 1)
                dve.wait_ge(S("x_v_ready"), i + 1)
                for b in range(2):
                    blk = dve.snap(nc.s_assert_within((p0 + i) * 2 + b, 0, NB - 1))
                    dst = Vx[:, ds(i * 2 + b, 1), :, :].rearrange("p o h d -> p (o h) d")
                    v.tensor_tensor(vf[:, b, :], ST[1][:, b * D:(b + 1) * D], bv_x[:, :], ALU.add) \
                        .then_inc(S("vf_made"), 1)
                    dve.wait_ge(S("vf_made"), i * 2 + (b + 1))
                    v.tensor_scalar(dst[:, :, 0:DH], vf[:, b, :].rearrange("p (h d) -> p h d", d=DH),
                                    real[:, ds(blk, 1)], None, ALU.mult).then_inc(S("vx_made"), 1)
                    v.tensor_copy(dst[:, :, DH:DH + 1], real[:, ds(blk, 1)].unsqueeze(1)
                                  .to_broadcast([P, HEADS, 1])).then_inc(S("vx_made"), 1)
                dve.wait_ge(S("vx_made"), i * 4 + 4)
            project_out("s")
            scaled_q("x", bq_x)
            dve_attention(dve, "x", n, n1)
            project_out("x")

            dve.wait_ge(S("logits"), 1)
            L = M[:, 0:QT * E].rearrange("p (t e) -> p t e", e=E)

            def bc(a):
                return a.unsqueeze(2).to_broadcast([P, QT, E])
            ch(v.tensor_tensor(lg[:, 0], L, br[:, :].unsqueeze(1).to_broadcast([P, QT, E]), ALU.add))
            ch(v.tensor_reduce(rsm[:, 0, :], lg[:, 0], AX.X, ALU.max))
            ch(v.tensor_tensor(lg[:, 1], lg[:, 0], bc(rsm[:, 0, :]), ALU.subtract))
            v.tensor_tensor(lg[:, 3], lg[:, 0], bc(rsm[:, 0, :]), ALU.is_equal).then_inc(S("shifted"), 1)
            dve.wait_ge(S("shifted"), 1)
            ch(v.tensor_tensor(lg[:, 3], lg[:, 3], down[:, NP - E:NP].unsqueeze(1).to_broadcast([P, QT, E]), ALU.mult))
            ch(v.tensor_reduce(rsm[:, 1, :], lg[:, 3], AX.X, ALU.max))
            ch(v.tensor_tensor(lg[:, 4], lg[:, 3], bc(rsm[:, 1, :]), ALU.is_equal))
            dve.wait_ge(S("router_exp"), 1)
            ch(v.tensor_reduce(rsm[:, 2, :], lg[:, 2], AX.X, ALU.add))
            ch(v.reciprocal(rsm[:, 3, :], rsm[:, 2, :]))
            v.tensor_tensor(lg[:, 5], lg[:, 4], bc(rsm[:, 3, :]), ALU.mult).then_inc(S("coef"), 1)
            dve.wait_ge(S("coef"), 1)
            for q in range(QT):
                dve.wait_ge(S("coefT"), q + 1)
                v.tensor_copy(coefT[:, :], M[0:E, 128:128 + P]).then_inc(S("coefT_copied"), 1)
                dve.wait_ge(S("y_all"), q + 1)
                dve.wait_ge(S("y_bias"), q + 1)
                ch(v.tensor_tensor(x[:, q, :], x[:, q, :], M[:, 256:256 + D], ALU.add))
                for e in range(E):
                    ins = v.scalar_tensor_tensor(out=x[:, q, :], in0=ST[q % 2][:, e * D:(e + 1) * D],
                                                 scalar=lg[:, 5, q, e:e + 1], in1=x[:, q, :],
                                                 op0=ALU.mult, op1=ALU.add)
                    if e + 1 < E:
                        ch(ins)
                ins.then_inc(S("f_res"), 1)
            layer_norm(dve, "f", ch)
            for q in range(QT):
                v.tensor_scalar(attn[:, q, :], x[:, q, :], mv[:, q, 0:1], rstd[:, q:q + 1],
                                ALU.subtract, ALU.mult).then_inc(S("out_done"), 1)

        @block.scalar
        def _(act):
            def std(a):
                act.wait_ge(S(a + "_var"), QT)
                act.wait_ge(S("cst"), 8)
                nc.scalar.activation(rstd[:, :], mv[:, :, 1], ACT.Sqrt, bias=eps[:, 0:1]).then_inc(S(a + "_std"), 1)

            act.preload_act_table(ACT.Exp)
            act.sem_inc(S("s_exp"), 2)
            act_attention(act, "s", SELF_PAIRS)
            std("s")
            act.wait_ge(S("steered"), 1)
            n = act.snap(act.value_load(steer[0:1, 1:2], min_val=MIN_PAIRS, max_val=NP))
            act.preload_act_table(ACT.Exp)
            act.sem_inc(S("x_exp"), 2)
            act_attention(act, "x", n)
            std("x")
            act.wait_ge(S("shifted"), 1)
            nc.scalar.activation(lg[:, 2], lg[:, 1], ACT.Exp).then_inc(S("router_exp"), 1)
            std("f")

        @block.tensor
        def _(pe):
            mmul = nc.tensor.matmul
            pe.wait_ge(S("in_x"), 16 * 7)
            for h in range(2):
                mm = mmul(ST[1][0:DH, h * 512:(h + 1) * 512], wk_s[:, :], xT[:, h * 512:(h + 1) * 512],
                          start=True, stop=True)
            mm.then_inc(S("s_k_ready"), 1)

            def project_q(a, w):
                for h in range(2):
                    mm = mmul(ST[0][:, h * 512:(h + 1) * 512], w[:, :], xT[:, h * 512:(h + 1) * 512],
                              start=True, stop=True)
                mm.then_inc(S(a + "_q_ready"), 1)

            project_q("s", wq_s)
            for b in range(Q // P):
                mm = mmul(M[:, b * DH:(b + 1) * DH], xT[:, b * P:(b + 1) * P], wv_s[:, :], start=True, stop=True)
            mm.then_inc(S("s_v_ready"), 1)
            pe.wait_ge(S("cst"), 8)
            pe.wait_ge(S("in_w"), 16 * 14)
            pe.wait_ge(S("vs_made"), 1)
            pe.wait_ge(S("krow"), 16 * (2 + SPLIT))
            pe.wait_ge(S("s_q_in"), 16 * 9)
            pe.wait_ge(S("k_in"), 16 * 3)
            pe.wait_ge(S("s_k_ev"), 1)
            pe.wait_ge(S("s_q_parts"), 5)
            pe.sem_inc(S("s_pv"), 2)
            pe_attention(pe, "s", SELF_PAIRS, SELF_PAIRS - 1, False)

            pe.wait_ge(S("s_normed"), NG)
            pe.wait_ge(S("mask_counts"), 1)
            for j in range(NB):
                mm = mmul(M[:, j:j + 1], acc[:, j * P:(j + 1) * P], ones[:, 0:1], start=True, stop=True)
            mm.then_inc(S("counted"), 1)
            pe.wait_ge(S("flags"), 1)
            mmul(M[:, 64:64 + 2 * NB], ones[:, :], lp[:, :], start=True, stop=True)
            nc.tensor.transpose(M[0:NB, 192:192 + P], cnt[:, :], ident[:, :]).then_inc(S("flag_sums"), 1)
            pe.wait_ge(S("steered"), 1)
            n = pe.snap(pe.value_load(steer[0:1, 1:2], min_val=MIN_PAIRS, max_val=NP))
            n1 = pe.snap(pe.value_load(steer[0:1, 3:4], min_val=MIN_PAIRS - 1, max_val=NP - 1))
            general = pe.snap(pe.value_load(steer[0:1, 2:3], min_val=0, max_val=1))
            with pe.Fori(0, n) as i:
                pe.wait_ge(S("ctx_in"), i * 16 + 16)
                pe.wait_ge(S("vx_made"), i * 4)
                mmul(ST[0][:, 0:PAIR], wk_x[:, :], ctxs[:, :], start=True, stop=True).then_inc(S("x_k_ready"), 1)
                for b in range(2):
                    mm = mmul(ST[1][:, b * D:(b + 1) * D], ctxs[:, b * P:(b + 1) * P], wv_x[:, :],
                              start=True, stop=True)
                mm.then_inc(S("x_v_ready"), 1)

            def project_out(a, w):
                pe.wait_ge(S(a + "_normed"), NG)
                if a == "s":
                    pe.wait_ge(S("vx_made"), n * 4)
                for q in range(QT):
                    mm = nc.tensor.transpose(ST[0][:, q * P:(q + 1) * P], attn[:, q, :], ident[:, :])
                mm.then_inc(S(a + "_aT"), 1)
                pe.wait_ge(S(a + "_aT_copied"), 1)
                for q in range(QT):
                    mm = mmul(ST[1][:, q * D:(q + 1) * D], aT[:, q * P:(q + 1) * P], w[:, :], start=True, stop=True)
                    if q % 4 == 3:
                        mm.then_inc(S(a + "_y"), 1)
                pe.wait_ge(S(a + "_x"), QT)
                for q in range(QT):
                    mm = nc.tensor.transpose(ST[0][:, q * P:(q + 1) * P], x[:, q, :], ident[:, :])
                mm.then_inc(S(a + "_xT"), 1)
                pe.wait_ge(S(a + "_xT_copied"), 1)

            project_out("s", wo_s)
            project_q("x", wq_x)
            pe.wait_ge(S("x_q_in"), 16 * 9)
            pe.wait_ge(S("x_q_parts"), 5)
            pe.sem_inc(S("x_pv"), 2)
            with pe.If(general == 1):
                pe_attention(pe, "x", n, n1, True)
            with pe.Else():
                pe_attention(pe, "x", n, n1, False)
            project_out("x", wo_x)

            for q in range(QT):
                mm = mmul(M[:, q * E:(q + 1) * E], xT[:, q * P:(q + 1) * P], wr[:, :], start=True, stop=True)
            mm.then_inc(S("logits"), 1)
            pe.wait_ge(S("bo2"), 32)
            for q in range(QT):
                if q >= 2:
                    pe.wait_ge(S("f_res"), q - 1)
                for h in range(2):
                    mm = mmul(ST[q % 2][:, h * 512:(h + 1) * 512], xT[:, q * P:(q + 1) * P],
                              we[:, 4 * h:4 * h + 4, :].rearrange("p e o -> p (e o)"), start=True, stop=True)
                mm.then_inc(S("y_all"), 1)
                pe.wait_ge(S("coef"), 1)
                if q:
                    pe.wait_ge(S("f_res"), q)
                nc.tensor.transpose(M[0:E, 128:128 + P], lg[:, 5, q, :], ident[:, :]).then_inc(S("coefT"), 1)
                pe.wait_ge(S("coefT_copied"), q + 1)
                mmul(M[:, 256:256 + D], coefT[:, :], be[:, :], start=True, stop=True).then_inc(S("y_bias"), 1)


def kernel(**inputs):
    import numpy as np
    import concourse.bacc as bacc
    from concourse.bass_utils import run_bass_kernel_spmd

    a = {k: np.asarray(v) for k, v in inputs.items()}
    x, c = a["x"][0], a["ctx_1024"][0]
    front = lambda m: np.concatenate([np.zeros((m.shape[0], FRONT), m.dtype), m], 1)
    laid = {
        "x": x, "xT": x.T, "ctxT": front(c.T), "mask": front(a["mask_SxS2_ik0"]),
        "wq_s": a["L0_attn_Wq"], "wk_s": a["L0_attn_Wk"], "wv_s": a["L0_attn_Wv"], "wo_s": a["L0_attn_Wo"],
        "bq_s": a["L0_attn_bq"], "bk_s": a["L0_attn_bk"], "bv_s": a["L0_attn_bv"], "bo_s": a["L0_attn_bo"],
        "wq_x": a["L0_xattn_Wq"].T, "wk_x": a["L0_xattn_Wk"].T, "wv_x": a["L0_xattn_Wv"].T,
        "wo_x": a["L0_xattn_Wo"].T,
        "bq_x": a["L0_xattn_bq"], "bk_x": a["L0_xattn_bk"], "bv_x": a["L0_xattn_bv"], "bo_x": a["L0_xattn_bo"],
        "wr": a["L0_ffn_router_w"].T, "br": a["L0_ffn_router_b"],
        "we": a["L0_ffn_expert_w"].transpose(2, 0, 1).reshape(D, E * D), "be": a["L0_ffn_expert_b"],
        "countdown": np.arange(NP, 0, -1).astype(np.float32),
    }
    nc = bacc.Bacc("TRN2", target_bir_lowering=False, num_devices=1)
    arrays, t = {}, {}
    for name, v in laid.items():
        v = np.ascontiguousarray(v)
        arrays["in_" + name] = v
        t[name] = nc.dram_tensor("in_" + name, v.shape, mybir.dt.from_np(v.dtype), kind="ExternalInput").ap()
    out = nc.dram_tensor("out_0", (Q, D), F32, kind="ExternalOutput").ap()
    decoder_layer(nc, t, out)
    r = run_bass_kernel_spmd(nc, [arrays], core_ids=[0])
    return r.results[0]["out_0"].reshape(1, Q, D)
```

```python
from contextlib import ExitStack
from functools import partial

import concourse.bass as bass
from concourse import mybir

F32 = mybir.dt.float32
BF16 = mybir.dt.bfloat16
I32 = mybir.dt.int32
U8 = mybir.dt.uint8
ALU = mybir.AluOpType
ACT = mybir.ActivationFunctionType
AX = mybir.AxisListType
ds = bass.ds

P = 128
D = 128
Q = 1024
QT = Q // P
HEADS = 16
DH = D // HEADS
GH = 2
NG = HEADS // GH
KEYS = 6404
PAIR = 256
NP = -(-KEYS // PAIR)
KPAD = NP * PAIR
FRONT = KPAD - KEYS
NB = KPAD // P
SELF_PAIRS = Q // PAIR
MIN_PAIRS = 3
SPLIT = 3
SROWS = SPLIT * SPLIT * DH
PEN = SROWS
MAXROW = SROWS + 1
KR = MAXROW + SPLIT
CH = GH * PAIR // P
NBANK = GH * QT * PAIR // 512
E = 8
EPS = 1e-5
SCALE = float(DH) ** -0.5
PENALTY = -(2.0 ** 100)
VW = DH + 1


def decoder_layer(nc, t, out):
    ctx = ExitStack()
    with ctx:
        def sb(name, shape, dt=F32):
            return ctx.enter_context(nc.sbuf_tensor(name, shape, dt))

        def ps(name, shape):
            return ctx.enter_context(nc.psum_tensor(name, shape, F32))

        def sem(name):
            return ctx.enter_context(nc.semaphore(name))

        def dram(name, shape, dt):
            return nc.dram_tensor(name, shape, dt, kind="Internal").ap()

        x = sb("x", [P, QT, D])
        xT = sb("xT", [P, Q])
        wq_s, wo_s = sb("wq_s", [P, D]), sb("wo_s", [P, D])
        wq_x, wk_x, wv_x, wo_x = (sb(n, [P, D]) for n in ("wq_x", "wk_x", "wv_x", "wo_x"))
        wk_s, wv_s = sb("wk_s", [P, DH]), sb("wv_s", [P, DH])
        bq_s, bq_x, bk_x = sb("bq_s", [P, 1]), sb("bq_x", [P, 1]), sb("bk_x", [P, 1])
        bk_s = sb("bk_s", [DH, 1])
        bv_s = sb("bv_s", [P, DH])
        bv_x = sb("bv_x", [P, D])
        bo = sb("bo", [P, D])
        ident = sb("ident", [P, P])
        penI = sb("penI", [P, P], BF16)
        ones = sb("ones", [P, P], BF16)
        zrow = sb("zrow", [P, 512], BF16)
        Qs = sb("Qs", [P, HEADS, Q], BF16)
        Kself = sb("Kself", [P, Q], BF16)
        Kx = sb("Kx", [P, 3, GH, KPAD], BF16)
        prob = sb("prob", [P, CH, Q])
        Vs = sb("Vs", [P, Q // P, VW])
        Vx = sb("Vx", [P, NB, HEADS, VW])
        vst = sb("vst", [P, 2, GH, VW])
        real = sb("real", [P, NB])
        ctxn = sb("ctxn", [P, PAIR])
        ctxs = sb("ctxs", [P, PAIR])
        kf = sb("kf", [P, PAIR])
        kr = sb("kr", [P, PAIR])
        vf = sb("vf", [P, 2, D])
        kp = sb("kp", [P, 2, SPLIT, PAIR], BF16)
        gint = sb("gint", [P, QT, PAIR], I32)
        grow = sb("grow", [P, QT, PAIR], BF16)
        gcol = sb("gcol", [P, QT, PAIR], BF16)
        mx = sb("mx", [P, 2, GH * QT])
        mxt = sb("mxt", [P, GH * QT])
        negm = sb("negm", [GH * QT, P])
        negr = sb("negr", [GH * QT, P])
        mxp = sb("mxp", [GH * QT, SPLIT, P], BF16)
        osb = sb("osb", [P, 512])
        rden = sb("rden", [P, 4, 2 * GH])
        attn = sb("attn", [P, QT, D])
        cnt = sb("cnt", [P, NB])
        lp = sb("lp", [P, 2 * NB], BF16)
        sm = sb("sm", [P, 2, NP])
        down = sb("down", [P, NP])
        steer = sb("steer", [1, 4], I32)
        sc1 = sb("sc1", [P, 8])
        penr = sb("penr", [NB, P], BF16)
        stat = sb("stat", [P, QT, 6])
        mv = sb("mv", [P, QT, 2])
        rstd = sb("rstd", [P, QT])
        eps = sb("eps", [P, 1])
        lg = sb("lg", [P, 6, QT, E])
        rsm = sb("rsm", [P, 4, QT])
        wr = sb("wr", [P, E])
        br = sb("br", [P, E])
        be = sb("be", [E, D])


        qf, qr = prob[:, 0, :], prob[:, 1, :]
        qp = prob[:, 2:4, :].bitcast(BF16)[:, :, :].rearrange("p a q -> p (a q)")[:, 0:SPLIT * Q] \
            .rearrange("p (a q) -> p a q", a=SPLIT)
        aT, coefT = prob[:, 0, :], prob[0:E, 1, :]
        kp8 = [m_[0:DH, h * 4:h * 4 + 4, :].rearrange("p a b -> p (a b)") for m_, h in ((grow, 0), (grow, 1), (gcol, 0))]
        kf8 = gint[0:DH, 0:4, :].rearrange("p a b -> p (a b)").bitcast(F32)
        kr8 = gint[0:DH, 4:8, :].rearrange("p a b -> p (a b)").bitcast(F32)
        maskI = [Kx[:, b, :, :].rearrange("p h k -> p (h k)").bitcast(I32) for b in range(2)]
        dead8 = Kx[:, 2, 0, 0:KPAD // 2].bitcast(U8)
        acc8 = Kx[:, 2, 0, KPAD // 2:KPAD].bitcast(U8)
        acc = Kx[:, 2, 1, :]
        we = Kx[:, 0, :, :].rearrange("p h k -> p (h k)")[:, 0:2 * E * D].bitcast(F32) \
            .rearrange("p (e o) -> p e o", e=E)

        qd = dram("qd", [SPLIT, D, Q], BF16)
        ksd = dram("ksd", [SPLIT * DH, Q], BF16)
        kd = dram("kd", [HEADS, SPLIT * DH, KPAD], BF16)
        tail = dram("tail", [1 + SPLIT, KPAD], BF16)

        ST = [ps(f"ST{n}", [P, Q]) for n in range(2)]
        SR_BANK = (0, 1, 2, 0, 1, 2, 0, 1)
        SR_BACK = (2, 2, 4, 3, 3, 3, 3, 3)
        SR = [ps(f"SR{n}", [P, 512]) for n in range(2)]
        O = ps("O", [P, 512])
        M = ps("M", [P, 512])
        SR.append(M)

        sems = {n_: sem(n_) for n_ in (
            "in_x in_r bo_added in_w cst0 cst q_out0 q_out1 q_out2 k_out k_in krow s_k_ready s_k_ev s_k_parts s_v_ready vs_ones vs_made "
            "mask_in0 mask_in1 mask_used mask_added mask_counts counted flags flag_sums steered pen_made "
            "ctx_in ctx_moved x_k_ready x_k_ev x_k_parts kd_out x_v_ready vf_made vx_made kx_in0 kx_in1 kx_in2 "
            "v_staged grow_in grow_ready grow_free gcol_in gcol_ready gcol_free dve_chain "
            "passed we_in logits shifted router_exp coef coefT coefT_copied y_all y_bias f_sum f_res f_stats f_var f_std "
            "out_done stored").split()}
        for a_ in "sx":
            for n_ in ("q_ready q_parts q_in0 q_in row_ready row_free mx mx_turned mx_copied mx_chain mx_parts "
                       "max_in0 max_in1 col_ready exp pv o_copied o_turned rden normed aT aT_copied y res "
                       "stats var std x xT xT_copied").split():
                sems[f"{a_}_{n_}"] = sem(f"{a_}_{n_}")

        def S(name):
            return sems[name]

        block = ctx.enter_context(nc.Block())

        def kstack(a, g, rows, hh, start, size):
            if a == "s":
                return Kself[0:rows, ds(start, size)]
            return Kx[0:rows, g % 3, hh, ds(start, size)]

        def loop(eng, start, end):
            if isinstance(end, int):
                yield from range(start, end)
            else:
                with eng.Fori(start, end) as i:
                    yield i

        def at(eng, value):
            return value if isinstance(value, int) else eng.snap(value)

        def wait_count(eng, semaphore, value):
            eng.wait_ge(semaphore, value)
            eng.sem_inc(S("passed"), 1)

        def pe_attention(pe, a, n, n1, general, beside=None):
            rows_r = SROWS if a == "s" else SROWS + 1

            def row_bank(g, U, i, j):
                pe.wait_ge(S(a + "_row_free"), U * NBANK + (j + 3 - SR_BACK[j]))
                hh = j // (NBANK // GH)
                for r in range(2):
                    qt = 2 * (j % (NBANK // GH)) + r
                    o = SR[SR_BANK[j]][:, r * PAIR:(r + 1) * PAIR]
                    mm = nc.tensor.matmul(o, Qs[0:rows_r, GH * g + hh, qt * P:(qt + 1) * P],
                                          kstack(a, g, rows_r, hh, i * PAIR, PAIR),
                                          start=True, stop=not general, skip_group_check=True)
                    if general:
                        mm = nc.tensor.matmul(o, penI[:, :], grow[:, qt, :], start=False, stop=True,
                                              skip_group_check=True)
                mm.then_inc(S(a + "_row_ready"), 1)

            def row_begin(U):
                if general:
                    pe.wait_ge(S("grow_ready"), U + 1)

            def row_end():
                if general:
                    pe.drain().then_inc(S("grow_free"), 1)

            def column(g, T, i, c):
                b, hh = c // GH, c % GH
                pe.wait_ge(S(a + "_exp"), T * CH + (c + 1))
                if general and c == 0:
                    pe.wait_ge(S("gcol_ready"), T + 1)
                for half in range(2):
                    mm = nc.tensor.matmul(ST[c % 2][:, half * 512:(half + 1) * 512],
                                          kstack(a, g, KR, hh, i * PAIR + b * P, P),
                                          Qs[0:KR, GH * g + hh, half * 512:(half + 1) * 512],
                                          start=True, stop=not general, skip_group_check=True)
                    if general:
                        for qt in range(4 * half, 4 * half + 4):
                            mm = nc.tensor.matmul(ST[c % 2][:, qt * P:(qt + 1) * P],
                                                  gcol[:, qt, b * P:(b + 1) * P], penI[:, :],
                                                  start=False, stop=(qt % 4 == 3),
                                                  skip_group_check=True)
                mm.then_inc(S(a + "_col_ready"), 1)
                if general and c == CH - 1:
                    pe.drain().then_inc(S("gcol_free"), 1)

            def values(T, i, b, back=0):
                pe.wait_ge(S(a + "_exp"), T * CH + (GH * b + GH + 2 - CH * back))
                if a == "x":
                    pe.wait_ge(S("v_staged"), T * 2 + (b + 1 - 2 * back))
                for hh in range(GH):
                    for half in range(2):
                        r = 32 * (2 * hh + half)
                        v = Vs[:, 2 * i + b, :] if a == "s" else vst[:, b, hh, :]
                        mm = nc.tensor.matmul(O[r:r + VW, :], v,
                                              prob[:, GH * b + hh, half * 512:(half + 1) * 512],
                                              start=False, stop=False, skip_group_check=True)
                mm.then_inc(S(a + "_pv"), 1)

            def clear_o(g):
                if g:
                    pe.wait_ge(S(a + "_o_copied"), g)
                nc.tensor.matmul(O[:, :], zrow[:, 0:P], zrow[:, :], start=True, stop=False,
                                 skip_group_check=True)

            def max_turn(g):
                pe.wait_ge(S(a + "_mx"), n1 * (2 * (g + 1)))
                if g:
                    pe.wait_ge(S(a + "_mx_copied"), g)
                if g >= 2:
                    pe.wait_ge(S(a + "_normed"), g - 1)
                nc.tensor.transpose(M[0:GH * QT, 0:P], mx[:, g % 2, :], ident[:, :]) \
                    .then_inc(S(a + "_mx_turned"), 1)

            def o_turn(g):
                pe.wait_ge(S(a + "_o_copied"), g + 1)
                pe.wait_ge(S(a + "_mx_copied"), min(g + 2, NG))
                if a == "s" and g == NG - 1:
                    pe.wait_ge(S("pen_made"), 1)
                if g:
                    pe.wait_ge(S(a + "_normed"), g)
                for t_ in range(4):
                    mm = nc.tensor.transpose(M[:, t_ * P:(t_ + 1) * P], osb[:, t_ * P:(t_ + 1) * P],
                                             ident[:, :])
                mm.then_inc(S(a + "_o_turned"), 1)

            def loaded(g):
                if g == 1:
                    pe.wait_ge(S(a + "_q_in"), 16 * 9)
                if a == "x":
                    pe.wait_ge(S(f"kx_in{g % 3}"), n * (4 * 16 * (g // 3 + 1)))

            loaded(0)
            row_begin(0)
            for j in range(NBANK):
                row_bank(0, 0, 0, j)
            row_end()
            for i in loop(pe, 1, n):
                row_begin(i)
                for j in range(NBANK):
                    row_bank(0, i, i, j)
                row_end()
            loaded(1)
            row_begin(n)
            for j in range(NBANK):
                if j == 2:
                    max_turn(0)
                    pe.wait_ge(S(a + "_mx_copied"), 1)
                row_bank(1, n, 0, j)
            row_end()

            def step(g, T, i, rg, ri, first=False, last=False):
                U = at(pe, T + n + 1) if rg < NG else None

                def rows(j):
                    if rg < NG:
                        row_bank(rg, U, ri, j)

                def before():
                    if not (first and g == 0):
                        values(T, (i - 1) % n if a == "s" else None, 1, back=1)

                if rg < NG:
                    row_begin(U)
                if first:
                    rows(0), rows(1), before(), rows(2)
                    pe.wait_ge(S(f"{a}_max_in{g % 2}"), 16 * SPLIT * (g // 2 + 1))
                    column(g, T, i, 0), rows(3), column(g, T, i, 1)
                elif last:
                    column(g, T, i, 0), rows(0), column(g, T, i, 1), rows(1)
                    if g + 1 < NG:
                        max_turn(g + 1)
                    before(), column(g, T, i, 2)
                    if g + 1 < NG:
                        pe.wait_ge(S(a + "_mx_copied"), g + 2)
                    rows(2), rows(3)
                else:
                    column(g, T, i, 0), rows(0), column(g, T, i, 1), rows(1)
                    if g:
                        pe.wait_ge(S(a + "_normed"), g)
                    rows(2), before(), rows(3)
                if not last:
                    column(g, T, i, 2)
                rows(4), rows(5), column(g, T, i, 3), rows(6), rows(7)
                if rg < NG:
                    row_end()
                if first:
                    clear_o(g)
                values(T, i, 0)
                if first and g:
                    if rg < NG:
                        pe.wait_ge(S(a + "_row_free"), U * NBANK + NBANK)
                    o_turn(g - 1)

            for g in range(NG):
                T0 = at(pe, n * g)
                step(g, T0, 0, g + 1, 1, first=True)
                for i in loop(pe, 1, n1):
                    step(g, at(pe, T0 + i), i, g + 1, i + 1)
                    if beside and g == NG - 1:
                        beside[i]()
                if g + 2 < NG:
                    loaded(g + 2)
                step(g, at(pe, T0 + n1), n1, g + 2, 0, last=True)
            values(at(pe, n * NG), n1 if a == "s" else None, 1, back=1)
            o_turn(NG - 1)

        def act_attention(act, a, n):
            def step(T):
                for c in range(CH):
                    act.wait_ge(S(a + "_col_ready"), T * CH + (c + 1))
                    if c % GH == 0:
                        act.wait_ge(S(a + "_pv"), T * 2 + (c // GH + 1))
                    nc.scalar.activation(prob[:, c, :], ST[c % 2][:, :], ACT.Exp).then_inc(S(a + "_exp"), 1)

            def copy_o(g):
                act.wait_ge(S(a + "_pv"), n * (2 * (g + 1)) + 2)
                if g:
                    act.wait_ge(S(a + "_o_turned"), g)
                nc.scalar.copy(osb[:, :], O[:, :]).then_inc(S(a + "_o_copied"), 1)

            for g in range(NG):
                T0 = at(act, n * g)
                if g:
                    copy_o(g - 1)
                step(T0)
                with act.Fori(1, n) as i:
                    step(at(act, T0 + i))
            copy_o(NG - 1)

        def dve_attention(dve, a, n, n1, ahead=None, beside=None):
            parts = [0]

            def row_max(g, U, j, first):
                dve.wait_ge(S(a + "_row_ready"), U * NBANK + (j + 1))
                o = mx[:, g % 2, 2 * j:2 * j + 2] if first else mxt[:, 2 * j:2 * j + 2]
                nc.vector.tensor_reduce(o, SR[SR_BANK[j]][:, :].rearrange("p (r k) -> p r k", r=2), AX.X,
                                        ALU.max).then_inc(S(a + "_row_free"), 1)

            def wait_mx(value):
                (dve.wait_ge if a == "s" else partial(wait_count, dve))(S(a + "_mx"), value)

            def running(g, part, reduced):
                dve.wait_ge(S(a + "_row_free"), reduced)
                nc.vector.tensor_tensor(mx[:, g % 2, part], mx[:, g % 2, part], mxt[:, part], ALU.max) \
                    .then_inc(S(a + "_mx"), 1)

            PART_A, PART_B = slice(0, 12), slice(12, GH * QT)

            def row_later(g, U, k2, second):
                if not second:
                    wait_mx(k2 - 3)
                elif g:
                    wait_mx(k2 - 2)
                row_max(g, U, 0, False)
                if not second:
                    running(g, PART_B, U * NBANK + 2)
                for j in range(1, NBANK):
                    if j == 6 and not second:
                        wait_mx(k2 - 2)
                    row_max(g, U, j, False)
                    if j == 6:
                        running(g, PART_A, U * NBANK + (6 + 2))

            def split_max(g):
                def chain(ins):
                    parts[0] += 1
                    ins.then_inc(S(a + "_mx_chain"), 1)
                    dve.wait_ge(S(a + "_mx_chain"), parts[0])

                dve.wait_ge(S(a + "_mx_turned"), g + 1)
                if g:
                    dve.wait_ge(S(f"{a}_max_in{(g - 1) % 2}"), 16 * SPLIT * ((g - 1) // 2 + 1))
                nc.vector.tensor_scalar(negm[:, :], M[0:GH * QT, 0:P], -1.0, None, ALU.mult) \
                    .then_inc(S(a + "_mx_copied"), 1)
                dve.wait_ge(S(a + "_mx_copied"), g + 1)
                chain(nc.vector.tensor_copy(mxp[:, 0, :], negm[:, :]))
                chain(nc.vector.tensor_tensor(negr[:, :], negm[:, :], mxp[:, 0, :], ALU.subtract))
                chain(nc.vector.tensor_copy(mxp[:, 1, :], negr[:, :]))
                chain(nc.vector.tensor_tensor(negm[:, :], negr[:, :], mxp[:, 1, :], ALU.subtract))
                nc.vector.tensor_copy(mxp[:, 2, :], negm[:, :]).then_inc(S(a + "_mx_parts"), 1)
                dve.wait_ge(S(a + "_mx_parts"), g + 1)

            def normalise(g):
                dve.wait_ge(S(a + "_o_turned"), g + 1)
                o = M[:, :].rearrange("p (t h f r) -> p t h f r", t=4, h=GH, f=2)
                nc.vector.reciprocal(rden[:, :, :], M[:, :].rearrange("p (t s r) -> p t s r", t=4, s=4)
                                     [:, :, :, DH]).then_inc(S(a + "_rden"), 1)
                dve.wait_ge(S(a + "_rden"), g + 1)
                rd = rden[:, :, :].rearrange("p t (h f) -> p t h f", h=GH)
                for hh in range(GH):
                    for half in range(2):
                        h0 = (GH * g + hh) * DH
                        ins = nc.vector.tensor_tensor(
                            attn[:, 4 * half:4 * half + 4, h0:h0 + DH], o[:, :, hh, half, 0:DH],
                            rd[:, :, hh, half].unsqueeze(2).to_broadcast([P, 4, DH]), ALU.mult)
                ins.then_inc(S(a + "_normed"), 1)

            dve.sem_inc(S(a + "_row_free"), 2)
            for j in range(NBANK):
                row_max(0, 0, j, True)
            row_later(0, 1, 2, True)
            for i in loop(dve, 2, n):
                row_later(0, i, at(dve, i * 2), False)
            for j in range(NBANK):
                row_max(1, n, j, True)
                if j == 0:
                    running(0, PART_B, n * NBANK + 2)
                if j == 1:
                    split_max(0)
            for g in range(NG):
                T0 = at(dve, n * g)
                done = at(dve, n1 * (2 * (g + 1)))
                if g + 1 < NG:
                    row_later(g + 1, at(dve, T0 + n + 1), done + 2, True)
                if ahead and g == NG - 1:
                    ahead()
                if g:
                    normalise(g - 1)
                if g + 1 < NG:
                    for i in loop(dve, 1, n1):
                        row_later(g + 1, at(dve, T0 + n + 1 + i), at(dve, done + 2 + i * 2), False)
                    U = at(dve, T0 + n + n)
                    if g + 2 >= NG:
                        running(g + 1, PART_B, U * NBANK + 2)
                        split_max(g + 1)
                    else:
                        for j in range(NBANK):
                            row_max(g + 2, U, j, True)
                            if j == 0:
                                running(g + 1, PART_B, U * NBANK + 2)
                            if j == 1:
                                split_max(g + 1)
            if beside:
                beside()
            normalise(NG - 1)

        def sp_max_rows(sp, a, g):
            sp.wait_ge(S(a + "_mx_parts"), g + 1)
            for k in range(SPLIT):
                sp.dma_start(Qs[MAXROW + k:MAXROW + k + 1, GH * g:GH * (g + 1), :]
                             .rearrange("o h (t f) -> o (h t) f", f=P),
                             mxp[:, k, :]).then_inc(S(f"{a}_max_in{g % 2}"), 16)

        def split3(e, src, rest, parts, chain):
            chain(e.tensor_copy(parts[0], src))
            chain(e.tensor_tensor(rest, src, parts[0], ALU.subtract))
            chain(e.tensor_copy(parts[1], rest))
            chain(e.tensor_tensor(src, rest, parts[1], ALU.subtract))
            chain(e.tensor_copy(parts[2], src))

        def chainer(eng, name):
            n_ = [0]

            def chain(ins):
                n_[0] += 1
                ins.then_inc(S(name), 1)
                eng.wait_ge(S(name), n_[0])
            return chain

        @block.sync
        def _(sp):
            def load(dst, src, name):
                sp.dma_start(dst, src).then_inc(S(name), 16)

            load(xT[:, :], t["xT"], "in_x")
            load(x[:, :, :], t["x"].rearrange("(t p) d -> p t d", p=P), "in_r")
            load(bo[:, :], t["bo_s"].rearrange("(o f) -> o f", o=1).to_broadcast([P, D]), "in_r")
            sp.wait_ge(S("cst"), 7)
            load(Qs[PEN:PEN + 1, :, :].rearrange("o h q -> o (h q)"), ones[:, :], "krow")
            for h in range(2):
                load(Kself[PEN:PEN + 1, h * 512:(h + 1) * 512], zrow[0:1, :], "krow")

            def load_mask(q):
                if q >= 2:
                    sp.wait_ge(S("mask_used"), 4 * (q - 1))
                sp.dma_start(maskI[q % 2], t["mask"][q * P:(q + 1) * P, :]).then_inc(S(f"mask_in{q % 2}"), 16)
            load_mask(0)

            def stack_q(a, beside=None):
                base = {"s": 0, "x": 1}[a]

                def spread(k, h0, h1, name):
                    for b in range(SPLIT):
                        r = (k * SPLIT + b) * DH
                        load(Qs[r:r + DH, h0:h1, :],
                             qd[k].rearrange("(h d) q -> d h q", d=DH)[:, h0:h1, :], a + name)

                def first_heads(k):
                    sp.wait_ge(S(f"q_out{k}"), 16 * (base + 1))
                    spread(k, 0, GH, "_q_in0")

                for k in range(SPLIT):
                    sp.wait_ge(S(a + "_q_parts"), 2 * k + 1)
                    load(qd[k], qp[:, k, :], f"q_out{k}")
                    if k:
                        first_heads(k - 1)
                first_heads(SPLIT - 1)
                if beside:
                    beside()
                for k in range(SPLIT):
                    spread(k, GH, HEADS, "_q_in")

            def stack_k():
                sp.wait_ge(S("s_k_parts"), 5)
                for b in range(SPLIT):
                    load(ksd[b * DH:(b + 1) * DH, :], kp8[b], "k_out")
                sp.wait_ge(S("k_out"), 48)
                for k in range(SPLIT):
                    load(Kself[k * SPLIT * DH:(k + 1) * SPLIT * DH, :], ksd[:, :], "k_in")
                load_mask(1)
            stack_q("s", stack_k)
            for n_, b_ in (("wo_s", wo_s), ("wq_x", wq_x), ("wk_x", wk_x), ("wv_x", wv_x), ("wo_x", wo_x)):
                load(b_[:, :], t[n_], "in_w")
            load(bq_x[:, :], t["bq_x"].rearrange("(p o) -> p o", o=1), "in_w")
            load(bk_x[:, :], t["bk_x"].rearrange("(p o) -> p o", o=1), "in_w")
            load(bv_x[:, :], t["bv_x"].rearrange("(o f) -> o f", o=1).to_broadcast([P, D]), "in_w")
            load(wr[:, :], t["wr"], "in_w")
            load(br[:, :], t["br"].rearrange("(o f) -> o f", o=1).to_broadcast([P, E]), "in_w")
            load(be[:, :], t["be"], "in_w")
            load(down[:, :], t["countdown"].rearrange("(o f) -> o f", o=1).to_broadcast([P, NP]), "in_w")
            for k in range(SPLIT):
                load(tail[1 + k, :].rearrange("(a b) -> a b", a=NB), ones[0:NB, :], "krow")
            sp.wait_ge(S("bo_added"), 1)
            load(bo[:, :], t["bo_x"].rearrange("(o f) -> o f", o=1).to_broadcast([P, D]), "in_w")
            for g in range(NG):
                sp_max_rows(sp, "s", g)
                if g + 2 < QT:
                    load_mask(g + 2)

            sp.wait_ge(S("steered"), 1)
            p0 = sp.snap(sp.value_load(steer[0:1, 0:1], min_val=0, max_val=NP - MIN_PAIRS))
            n = sp.snap(sp.value_load(steer[0:1, 1:2], min_val=MIN_PAIRS, max_val=NP))
            sp.wait_ge(S("pen_made"), 1)
            load(tail[0, :].rearrange("(a b) -> a b", a=NB), penr[:, :], "krow")
            def k_parts_out(i):
                wait_count(sp, S("x_k_parts"), i * 5 + 5)
                wait_count(sp, S("kd_out"), i * 48 + 48)
                for b in range(SPLIT):
                    sp.dma_start(kd[:, b * DH:(b + 1) * DH, ds(i * PAIR, PAIR)],
                                 kp[:, ds(i % 2, 1), b, :].rearrange("p o k -> p (o k)")) \
                        .then_inc(S("kd_out"), 16)

            with sp.Fori(0, n) as i:
                k_parts_out(i)
            wait_count(sp, S("kd_out"), n * 48 + 48)
            sp.wait_ge(S("krow"), 16 * (3 + SPLIT + 1))

            def load_k(g):
                if g >= 3:
                    wait_count(sp, S("x_pv"), n * (2 * (g - 2)) + 2)
                with sp.Fori(0, n) as i:
                    p = sp.snap(nc.s_assert_within(p0 + i, 0, NP - 1))
                    for k in range(SPLIT):
                        sp.dma_start(Kx[k * SPLIT * DH:(k + 1) * SPLIT * DH, g % 3, :, ds(i * PAIR, PAIR)],
                                     kd[GH * g:GH * (g + 1), :, ds(i * PAIR, PAIR)].rearrange("h r k -> r h k")) \
                            .then_inc(S(f"kx_in{g % 3}"), 16)
                    sp.dma_start(Kx[PEN:KR, g % 3, :, ds(i * PAIR, PAIR)],
                                 tail[:, ds(p * PAIR, PAIR)].rearrange("r (o k) -> r o k", o=1)
                                 .to_broadcast([1 + SPLIT, GH, PAIR])) \
                        .then_inc(S(f"kx_in{g % 3}"), 16)

            sp.wait_ge(S("counted"), 1)
            load_k(0)
            stack_q("x")
            load_k(1)
            load_k(2)
            for g in range(NG):
                sp_max_rows(sp, "x", g)
                if g >= 1 and g + 2 < NG:
                    load_k(g + 2)
            sp.wait_ge(S("x_normed"), NG)
            load(we, t["we"].rearrange("d (e o) -> d e o", e=E), "we_in")
            for q in range(QT):
                sp.wait_ge(S("out_done"), q + 1)
                load(out.rearrange("(t p) d -> p t d", p=P)[:, q, :], attn[:, q, :], "stored")
            sp.wait_ge(S("stored"), 16 * QT)

        @block.gpsimd
        def _(pool):
            g_ = nc.gpsimd
            g_.memset(ident[:, :], 0.0).then_inc(S("cst0"), 1)
            g_.memset(penI[:, :], 0.0).then_inc(S("cst0"), 1)
            g_.memset(real[:, :], 1.0).then_inc(S("cst0"), 1)
            pool.wait_ge(S("cst0"), 3)
            g_.affine_select(out=ident[:, :], in_=ident[:, :], compare_op=ALU.not_equal, fill=1.0, base=0,
                             pattern=[[-1, P]], channel_multiplier=1).then_inc(S("cst"), 1)
            g_.affine_select(out=penI[:, :], in_=penI[:, :], compare_op=ALU.not_equal, fill=PENALTY, base=0,
                             pattern=[[-1, P]], channel_multiplier=1).then_inc(S("cst"), 1)
            g_.affine_select(out=real[:, :], in_=real[:, :], compare_op=ALU.is_ge, fill=0.0, base=-FRONT,
                             pattern=[[P, NB]], channel_multiplier=1).then_inc(S("cst"), 1)
            g_.memset(ones[:, :], 1.0).then_inc(S("cst"), 1)
            g_.memset(zrow[:, :], 0.0).then_inc(S("cst"), 1)
            g_.memset(eps[:, :], EPS).then_inc(S("cst"), 1)
            half = KPAD // 4

            for q in range(QT):
                dst = acc8 if q == 0 else dead8
                pool.wait_ge(S(f"mask_in{q % 2}"), 16 * (q // 2 + 1))
                for c in range(4):
                    w = slice(c * half, (c + 1) * half)
                    g_.tensor_scalar(dst[:, w], maskI[q % 2][:, w], 0.0, None, ALU.is_equal) \
                        .then_inc(S("mask_used"), 1)
                pool.wait_ge(S("mask_used"), 4 * (q + 1))
                if q:
                    g_.tensor_tensor(acc8.bitcast(I32), acc8.bitcast(I32), dead8.bitcast(I32), ALU.add) \
                        .then_inc(S("mask_added"), 1)
                    pool.wait_ge(S("mask_added"), q)
            pool.wait_ge(S("steered"), 1)
            n = pool.snap(pool.value_load(steer[0:1, 1:2], min_val=MIN_PAIRS, max_val=NP))
            n1 = pool.snap(pool.value_load(steer[0:1, 3:4], min_val=MIN_PAIRS - 1, max_val=NP - 1))
            general = pool.snap(pool.value_load(steer[0:1, 2:3], min_val=0, max_val=1))
            p0 = pool.snap(pool.value_load(steer[0:1, 0:1], min_val=0, max_val=NP - MIN_PAIRS))
            pool.sem_inc(S("ctx_moved"), 1)
            with pool.Fori(0, n) as i:
                p = pool.snap(nc.s_assert_within(p0 + i, 0, NP - 1))
                wait_count(pool, S("ctx_moved"), i + 1)
                pool.dma_start(ctxn[:, :], t["ctxT"][:, ds(p * PAIR, PAIR)]).then_inc(S("ctx_in"), 16)
            def stage_v(g, T, i, b):
                wait_count(pool, S("x_pv"), T * 2 + (b + 1))
                g_.tensor_copy(vst[:, b, :, :], Vx[:, ds(i * 2 + b, 1), GH * g:GH * (g + 1), :]
                               .rearrange("p o h d -> p (o h) d")).then_inc(S("v_staged"), 1)

            def gen_fetch(dst, view, U, i):
                wait_count(pool, S(view + "_free"), U + 1)
                pool.dma_start(gint[:, :, :], t["mask"].rearrange("(t p) k -> p t k", p=P)
                               [:, :, ds(i * PAIR, PAIR)]).then_inc(S(view + "_in"), 16)
                wait_count(pool, S(view + "_in"), U * 16 + 16)
                g_.tensor_scalar(dst[:, :, :], gint[:, :, :], 0.0, None, ALU.is_equal) \
                    .then_inc(S(view + "_ready"), 1)
                wait_count(pool, S(view + "_ready"), U + 1)

            def stream(gen):
                if gen:
                    pool.sem_inc(S("grow_free"), 1)
                    pool.sem_inc(S("gcol_free"), 1)
                    with pool.Fori(0, n) as i:
                        gen_fetch(grow, "grow", i, i)
                    gen_fetch(grow, "grow", n, 0)

                def step(g, T, i, gr, ir):
                    if gen:
                        gen_fetch(gcol, "gcol", T, i)
                        if gr < NG:
                            gen_fetch(grow, "grow", pool.snap(T + n + 1), ir)
                    stage_v(g, T, i, 0)
                    stage_v(g, T, i, 1)

                for g in range(NG):
                    T0 = at(pool, n * g)
                    with pool.Fori(0, n1) as i:
                        step(g, pool.snap(T0 + i), i, g + 1, i + 1)
                    step(g, pool.snap(T0 + n1), n1, g + 2, 0)

            wait_count(pool, S("vx_made"), n * 4)
            with pool.If(general == 1):
                stream(True)
            with pool.Else():
                stream(False)

        def layer_norm(dve, a, chain):
            dve.wait_ge(S(a + "_res"), QT)
            for q in range(QT):
                nc.vector.bn_stats(stat[:, q, :], x[:, q, :]).then_inc(S(a + "_stats"), 1)
            for q in range(QT):
                dve.wait_ge(S(a + "_stats"), q + 1)
                nc.vector.bn_aggr(mv[:, q, :], stat[:, q, :]).then_inc(S(a + "_var"), 1)
            dve.wait_ge(S(a + "_std"), 1)
            chain(nc.vector.reciprocal(rstd[:, :], rstd[:, :]))

        @block.vector
        def _(dve):
            v = nc.vector
            ch = chainer(dve, "dve_chain")
            v.memset(Kself[64:96, :], 1.0).then_inc(S("cst"), 1)
            v.memset(Vs[:, :, :], 1.0).then_inc(S("vs_ones"), 1)

            def scaled_q(a, bq):
                dve.wait_ge(S(a + "_q_ready"), 1)
                dve.wait_ge(S("in_x" if a == "s" else "in_w"), 16 * (7 if a == "s" else 13))
                ch(v.tensor_scalar(qf, ST[0][:, :], bq[:, 0:1], SCALE, ALU.add, ALU.mult))
                n_ = [0]

                def c2(ins):
                    n_[0] += 1
                    ins.then_inc(S(a + "_q_parts"), 1)
                    dve.wait_ge(S(a + "_q_parts"), n_[0])
                split3(v, qf, qr, [qp[:, b, :] for b in range(SPLIT)], c2)

            scaled_q("s", bq_s)
            dve.wait_ge(S("s_k_ready"), 1)
            v.tensor_scalar(kf8, ST[1][0:DH, :], bk_s[:, 0:1], None, ALU.add).then_inc(S("s_k_ev"), 1)
            dve.wait_ge(S("s_k_ev"), 1)
            split3(v, kf8, kr8, [kp8[b] for b in range(SPLIT)], chainer(dve, "s_k_parts"))
            dve.wait_ge(S("s_v_ready"), 1)
            dve.wait_ge(S("vs_ones"), 1)
            v.tensor_tensor(Vs[:, :, 0:DH], M[:, 0:QT * DH].rearrange("p (b d) -> p b d", d=DH),
                            bv_s[:, :].unsqueeze(1).to_broadcast([P, QT, DH]), ALU.add) \
                .then_inc(S("vs_made"), 1)

            dve.wait_ge(S("in_r"), 32)
            add_bo = lambda: v.tensor_tensor(x[:, :, :], x[:, :, :], bo[:, :].unsqueeze(1)
                                             .to_broadcast([P, QT, D]), ALU.add)
            add_bo().then_inc(S("bo_added"), 1)
            dve.wait_ge(S("bo_added"), 1)
            def mask_counts():
                dve.wait_ge(S("mask_added"), QT - 1)
                for c in range(4):
                    w = slice(c * KPAD // 4, (c + 1) * KPAD // 4)
                    v.tensor_copy(acc[:, w], acc8[:, w]).then_inc(S("mask_counts"), 1)

            def steering():
                dve.wait_ge(S("counted"), 1)
                ch(v.tensor_copy(cnt[:, :], M[:, 0:NB]))
                ch(v.tensor_scalar(lp[:, 0:NB], cnt[:, :], float(Q), None, ALU.is_lt))
                v.scalar_tensor_tensor(out=lp[:, NB:2 * NB], in0=cnt[:, :], scalar=0.0, in1=lp[:, 0:NB],
                                       op0=ALU.is_gt, op1=ALU.mult).then_inc(S("flags"), 1)
                dve.wait_ge(S("flag_sums"), 1)
                ch(v.tensor_reduce(sm[:, 0, :], M[:, 64:64 + NB].rearrange("p (k b) -> p k b", b=2), AX.X, ALU.max))
                ch(v.tensor_reduce(sc1[:, 1:2], M[:, 64 + NB:64 + 2 * NB], AX.X, ALU.max))
                ch(v.tensor_scalar(sm[:, 0, :], sm[:, 0, :], 0.0, None, ALU.is_gt))
                dve.wait_ge(S("in_w"), 16 * 13)
                ch(v.tensor_tensor(sm[:, 1, :], sm[:, 0, :], down[:, :], ALU.mult))
                ch(v.tensor_reduce(sc1[:, 2:3], sm[:, 1, :], AX.X, ALU.max))
                ch(v.tensor_scalar(sc1[:, 3:4], sc1[:, 2:3], 0.0, None, ALU.is_equal))
                ch(v.tensor_scalar(sc1[:, 4:5], sc1[:, 1:2], 0.0, None, ALU.is_gt))
                ch(v.tensor_tensor(sc1[:, 5:6], sc1[:, 3:4], sc1[:, 4:5], ALU.max))
                ch(v.tensor_scalar(sc1[:, 6:7], sc1[:, 5:6], float(NP), None, ALU.mult))
                ch(v.tensor_tensor(sc1[:, 6:7], sc1[:, 6:7], sc1[:, 2:3], ALU.max))
                ch(v.tensor_scalar(sc1[:, 6:7], sc1[:, 6:7], float(MIN_PAIRS), None, ALU.max))
                ch(v.tensor_scalar(sc1[:, 7:8], sc1[:, 6:7], -1.0, float(NP), ALU.mult, ALU.add))
                ch(v.tensor_copy(steer[0:1, 0:1], sc1[0:1, 7:8]))
                ch(v.tensor_copy(steer[0:1, 1:2], sc1[0:1, 6:7]))
                ch(v.tensor_scalar(steer[0:1, 3:4], sc1[0:1, 6:7], -1.0, None, ALU.add))
                v.tensor_copy(steer[0:1, 2:3], sc1[0:1, 5:6]).then_inc(S("steered"), 1)
                ch(v.tensor_scalar(sc1[:, 0:1], sc1[:, 5:6], -PENALTY, PENALTY, ALU.mult, ALU.add))
                v.tensor_scalar(penr[:, :], M[0:NB, 192:192 + P], float(Q), sc1[0:NB, 0:1], ALU.is_equal,
                                ALU.mult).then_inc(S("pen_made"), 1)

            dve_attention(dve, "s", SELF_PAIRS, SELF_PAIRS - 1, mask_counts, steering)

            def project_out(a):
                dve.wait_ge(S(a + "_aT"), 1)
                v.tensor_copy(aT, ST[0][:, :]).then_inc(S(a + "_aT_copied"), 1)
                for h in range(2):
                    dve.wait_ge(S(a + "_y"), h + 1)
                    w = slice(4 * h, 4 * h + 4)
                    v.tensor_tensor(x[:, w, :], x[:, w, :], ST[1][:, h * 512:(h + 1) * 512]
                                    .rearrange("p (t d) -> p t d", d=D), ALU.add).then_inc(S(a + "_res"), 4)
                layer_norm(dve, a, ch)
                for q in range(QT):
                    v.tensor_scalar(x[:, q, :], x[:, q, :], mv[:, q, 0:1], rstd[:, q:q + 1],
                                    ALU.subtract, ALU.mult).then_inc(S(a + "_x"), 1)
                dve.wait_ge(S(a + "_xT"), 1)
                v.tensor_copy(xT[:, :], ST[0][:, :]).then_inc(S(a + "_xT_copied"), 1)

            dve.wait_ge(S("pen_made"), 1)
            n = dve.snap(dve.value_load(steer[0:1, 1:2], min_val=MIN_PAIRS, max_val=NP))
            n1 = dve.snap(dve.value_load(steer[0:1, 3:4], min_val=MIN_PAIRS - 1, max_val=NP - 1))
            p0 = dve.snap(dve.value_load(steer[0:1, 0:1], min_val=0, max_val=NP - MIN_PAIRS))
            dve.sem_inc(S("kd_out"), 48)
            with dve.Fori(0, n) as i:
                dve.wait_ge(S("x_v_ready"), i + 1)
                for b in range(2):
                    blk = dve.snap(nc.s_assert_within((p0 + i) * 2 + b, 0, NB - 1))
                    dst = Vx[:, ds(i * 2 + b, 1), :, :].rearrange("p o h d -> p (o h) d")
                    v.tensor_tensor(vf[:, b, :], ST[1][:, b * D:(b + 1) * D], bv_x[:, :], ALU.add) \
                        .then_inc(S("vf_made"), 1)
                    dve.wait_ge(S("vf_made"), i * 2 + (b + 1))
                    v.tensor_scalar(dst[:, :, 0:DH], vf[:, b, :].rearrange("p (h d) -> p h d", d=DH),
                                    real[:, ds(blk, 1)], None, ALU.mult).then_inc(S("vx_made"), 1)
                    v.tensor_copy(dst[:, :, DH:DH + 1], real[:, ds(blk, 1)].unsqueeze(1)
                                  .to_broadcast([P, HEADS, 1])).then_inc(S("vx_made"), 1)
                c5 = dve.snap(i * 5)
                k_ = [0]

                def part(ins):
                    k_[0] += 1
                    ins.then_inc(S("x_k_parts"), 1)
                    wait_count(dve, S("x_k_parts"), c5 + k_[0])
                wait_count(dve, S("x_k_ev"), i + 1)
                wait_count(dve, S("kd_out"), i * 48)
                half = dve.snap(i % 2)
                split3(v, kf[:, :], kr[:, :], [kp[:, ds(half, 1), b, :].rearrange("p o k -> p (o k)")
                                               for b in range(SPLIT)], part)
                dve.wait_ge(S("vx_made"), i * 4 + 4)
            project_out("s")
            scaled_q("x", bq_x)
            dve.wait_ge(S("in_w"), 16 * 13)
            ch(add_bo())
            dve_attention(dve, "x", n, n1)
            project_out("x")

            dve.wait_ge(S("logits"), 1)
            L = M[:, 0:QT * E].rearrange("p (t e) -> p t e", e=E)

            def bc(a):
                return a.unsqueeze(2).to_broadcast([P, QT, E])
            ch(v.tensor_tensor(lg[:, 0], L, br[:, :].unsqueeze(1).to_broadcast([P, QT, E]), ALU.add))
            ch(v.tensor_reduce(rsm[:, 0, :], lg[:, 0], AX.X, ALU.max))
            ch(v.tensor_tensor(lg[:, 1], lg[:, 0], bc(rsm[:, 0, :]), ALU.subtract))
            v.tensor_tensor(lg[:, 3], lg[:, 0], bc(rsm[:, 0, :]), ALU.is_equal).then_inc(S("shifted"), 1)
            dve.wait_ge(S("shifted"), 1)
            ch(v.tensor_tensor(lg[:, 3], lg[:, 3], down[:, NP - E:NP].unsqueeze(1).to_broadcast([P, QT, E]), ALU.mult))
            ch(v.tensor_reduce(rsm[:, 1, :], lg[:, 3], AX.X, ALU.max))
            ch(v.tensor_tensor(lg[:, 4], lg[:, 3], bc(rsm[:, 1, :]), ALU.is_equal))
            dve.wait_ge(S("router_exp"), 1)
            ch(v.tensor_reduce(rsm[:, 2, :], lg[:, 2], AX.X, ALU.add))
            ch(v.reciprocal(rsm[:, 3, :], rsm[:, 2, :]))
            v.tensor_tensor(lg[:, 5], lg[:, 4], bc(rsm[:, 3, :]), ALU.mult).then_inc(S("coef"), 1)
            for h in range(2):
                dve.wait_ge(S("y_bias"), h + 1)
                w = slice(4 * h, 4 * h + 4)
                ch(v.tensor_tensor(x[:, w, :], x[:, w, :], (M if h else O)[:, :]
                                   .rearrange("p (t d) -> p t d", d=D), ALU.add))
            done = 0
            for u in range(0, 2 * QT, 2):
                dve.wait_ge(S("y_all"), u + 2)
                for e in range(E // 2):
                    for r in range(2):
                        q = 2 * (u // 4) + r
                        if done >= 2 and not (e == 0 and u % 4 == 0):
                            dve.wait_ge(S("f_sum"), done - 1)
                        col = 4 * ((u // 2) % 2) + e
                        v.scalar_tensor_tensor(
                            out=x[:, q, :], in0=ST[(u // 2) % 2][:, r * 512 + e * D:r * 512 + (e + 1) * D],
                            scalar=lg[:, 5, q, col:col + 1], in1=x[:, q, :],
                            op0=ALU.mult, op1=ALU.add).then_inc(S("f_sum"), 1)
                        done += 1
            dve.wait_ge(S("f_sum"), done)
            dve.sem_inc(S("f_res"), QT)
            layer_norm(dve, "f", ch)
            for q in range(QT):
                v.tensor_scalar(attn[:, q, :], x[:, q, :], mv[:, q, 0:1], rstd[:, q:q + 1],
                                ALU.subtract, ALU.mult).then_inc(S("out_done"), 1)

        @block.scalar
        def _(act):
            def std(a):
                act.wait_ge(S(a + "_var"), QT)
                act.wait_ge(S("cst"), 7)
                nc.scalar.activation(rstd[:, :], mv[:, :, 1], ACT.Sqrt, bias=eps[:, 0:1]).then_inc(S(a + "_std"), 1)

            act.dma_start(wq_s[:, :], t["wq_s"]).then_inc(S("in_x"), 16)
            act.dma_start(wk_s[:, :], t["wk_s"]).then_inc(S("in_x"), 16)
            act.dma_start(wv_s[:, :], t["wv_s"]).then_inc(S("in_x"), 16)
            act.dma_start(bq_s[:, :], t["bq_s"].rearrange("(p o) -> p o", o=1)).then_inc(S("in_x"), 16)
            act.dma_start(bk_s[:, :], t["bk_s"].rearrange("(p o) -> p o", o=1)).then_inc(S("in_x"), 16)
            act.dma_start(bv_s[:, :], t["bv_s"].rearrange("(o f) -> o f", o=1).to_broadcast([P, DH])) \
                .then_inc(S("in_x"), 16)
            act.preload_act_table(ACT.Exp)
            act.sem_inc(S("s_exp"), 2)
            act_attention(act, "s", SELF_PAIRS)
            act.wait_ge(S("in_w"), 16 * 13)
            act.wait_ge(S("steered"), 1)
            n = act.snap(act.value_load(steer[0:1, 1:2], min_val=MIN_PAIRS, max_val=NP))
            with act.Fori(0, n) as i:
                act.wait_ge(S("ctx_in"), i * 16 + 16)
                act.wait_ge(S("x_v_ready"), i)
                nc.scalar.copy(ctxs[:, :], ctxn[:, :]).then_inc(S("ctx_moved"), 1)
                act.wait_ge(S("x_k_ready"), i + 1)
                act.wait_ge(S("x_k_parts"), i * 5)
                nc.scalar.activation(kf[:, :], ST[0][:, 0:PAIR], ACT.Identity, bias=bk_x[:, 0:1]) \
                    .then_inc(S("x_k_ev"), 1)
            std("s")
            act.preload_act_table(ACT.Exp)
            act.sem_inc(S("x_exp"), 2)
            act_attention(act, "x", n)
            std("x")
            act.wait_ge(S("shifted"), 1)
            nc.scalar.activation(lg[:, 2], lg[:, 1], ACT.Exp).then_inc(S("router_exp"), 1)
            act.wait_ge(S("coefT"), 1)
            for h in range(2):
                nc.scalar.copy(coefT[:, h * 512:(h + 1) * 512], SR[h][0:E, :]).then_inc(S("coefT_copied"), 1)
            std("f")

        @block.tensor
        def _(pe):
            mmul = nc.tensor.matmul
            pe.wait_ge(S("in_x"), 16 * 7)
            def project_q(a, w):
                for h in range(2):
                    mm = mmul(ST[0][:, h * 512:(h + 1) * 512], w[:, :], xT[:, h * 512:(h + 1) * 512],
                              start=True, stop=True)
                mm.then_inc(S(a + "_q_ready"), 1)

            project_q("s", wq_s)
            for h in range(2):
                mm = mmul(ST[1][0:DH, h * 512:(h + 1) * 512], wk_s[:, :], xT[:, h * 512:(h + 1) * 512],
                          start=True, stop=True)
            mm.then_inc(S("s_k_ready"), 1)
            for b in range(Q // P):
                mm = mmul(M[:, b * DH:(b + 1) * DH], xT[:, b * P:(b + 1) * P], wv_s[:, :], start=True, stop=True)
            mm.then_inc(S("s_v_ready"), 1)
            pe.wait_ge(S("cst"), 7)
            pe.wait_ge(S("vs_made"), 1)
            pe.wait_ge(S("krow"), 16 * 3)
            pe.wait_ge(S("s_q_in0"), 16 * 9)
            pe.wait_ge(S("k_in"), 16 * 3)
            pe.wait_ge(S("s_k_ev"), 1)
            pe.wait_ge(S("s_q_parts"), 5)
            pe.sem_inc(S("s_pv"), 2)

            def count_dead():
                pe.wait_ge(S("s_normed"), NG - 1)
                pe.wait_ge(S("mask_counts"), 4)
                for j in range(NB):
                    mm = mmul(M[:, j:j + 1], acc[:, j * P:(j + 1) * P], ones[:, 0:1], start=True, stop=True)
                mm.then_inc(S("counted"), 1)

            def sum_flags():
                pe.wait_ge(S("flags"), 1)
                mmul(M[:, 64:64 + 2 * NB], ones[:, :], lp[:, :], start=True, stop=True)
                nc.tensor.transpose(M[0:NB, 192:192 + P], cnt[:, :], ident[:, :]).then_inc(S("flag_sums"), 1)

            pe_attention(pe, "s", SELF_PAIRS, SELF_PAIRS - 1, False, {1: count_dead, 2: sum_flags})

            pe.wait_ge(S("steered"), 1)
            n = pe.snap(pe.value_load(steer[0:1, 1:2], min_val=MIN_PAIRS, max_val=NP))
            n1 = pe.snap(pe.value_load(steer[0:1, 3:4], min_val=MIN_PAIRS - 1, max_val=NP - 1))
            general = pe.snap(pe.value_load(steer[0:1, 2:3], min_val=0, max_val=1))
            pe.wait_ge(S("in_w"), 16 * 13)
            with pe.Fori(0, n) as i:
                pe.wait_ge(S("ctx_moved"), i + 2)
                pe.wait_ge(S("x_k_ev"), i)
                mmul(ST[0][:, 0:PAIR], wk_x[:, :], ctxs[:, :], start=True, stop=True).then_inc(S("x_k_ready"), 1)
                pe.wait_ge(S("vx_made"), i * 4)
                for b in range(2):
                    mm = mmul(ST[1][:, b * D:(b + 1) * D], ctxs[:, b * P:(b + 1) * P], wv_x[:, :],
                              start=True, stop=True)
                mm.then_inc(S("x_v_ready"), 1)

            def project_out(a, w):
                pe.wait_ge(S(a + "_normed"), NG)
                if a == "s":
                    pe.wait_ge(S("vx_made"), n * 4)
                    pe.wait_ge(S("x_k_ev"), n)
                for q in range(QT):
                    mm = nc.tensor.transpose(ST[0][:, q * P:(q + 1) * P], attn[:, q, :], ident[:, :])
                mm.then_inc(S(a + "_aT"), 1)
                pe.wait_ge(S(a + "_aT_copied"), 1)
                for q in range(QT):
                    mm = mmul(ST[1][:, q * D:(q + 1) * D], aT[:, q * P:(q + 1) * P], w[:, :], start=True, stop=True)
                    if q % 4 == 3:
                        mm.then_inc(S(a + "_y"), 1)
                pe.wait_ge(S(a + "_x"), QT)
                for q in range(QT):
                    mm = nc.tensor.transpose(ST[0][:, q * P:(q + 1) * P], x[:, q, :], ident[:, :])
                mm.then_inc(S(a + "_xT"), 1)
                pe.wait_ge(S(a + "_xT_copied"), 1)

            project_out("s", wo_s)
            project_q("x", wq_x)
            pe.wait_ge(S("x_q_in0"), 16 * 9)
            pe.wait_ge(S("x_q_parts"), 5)
            pe.sem_inc(S("x_pv"), 2)
            with pe.If(general == 1):
                pe_attention(pe, "x", n, n1, True)
            with pe.Else():
                pe_attention(pe, "x", n, n1, False)
            project_out("x", wo_x)

            for q in range(QT):
                mm = mmul(M[:, q * E:(q + 1) * E], xT[:, q * P:(q + 1) * P], wr[:, :], start=True, stop=True)
            mm.then_inc(S("logits"), 1)
            pe.wait_ge(S("we_in"), 16)
            for u in range(2 * QT):
                if u >= 4:
                    pe.wait_ge(S("f_sum"), 8 * (u // 2 - 1))
                q, h = 2 * (u // 4) + u % 2, (u // 2) % 2
                mmul(ST[h][:, (u % 2) * 512:(u % 2 + 1) * 512], xT[:, q * P:(q + 1) * P],
                     we[:, 4 * h:4 * h + 4, :].rearrange("p e o -> p (e o)"), start=True, stop=True) \
                    .then_inc(S("y_all"), 1)
                if u == 3:
                    pe.wait_ge(S("coef"), 1)
                    for q in range(QT):
                        mm = nc.tensor.transpose(SR[q // 4][0:E, (q % 4) * P:(q % 4 + 1) * P], lg[:, 5, q, :],
                                                 ident[:, :])
                    mm.then_inc(S("coefT"), 1)
                    pe.wait_ge(S("coefT_copied"), 2)
                    for q in range(QT):
                        o = (M if q >= 4 else O)[:, (q % 4) * D:(q % 4 + 1) * D]
                        mm = mmul(o, coefT[:, q * P:(q + 1) * P], be[:, :], start=True, stop=True)
                        if q % 4 == 3:
                            mm.then_inc(S("y_bias"), 1)


def kernel(**inputs):
    import numpy as np
    import concourse.bacc as bacc
    from concourse.bass_utils import run_bass_kernel_spmd

    a = {k: np.asarray(v) for k, v in inputs.items()}
    x, c = a["x"][0], a["ctx_1024"][0]
    front = lambda m: np.concatenate([np.zeros((m.shape[0], FRONT), m.dtype), m], 1)
    laid = {
        "x": x, "xT": x.T, "ctxT": front(c.T), "mask": front(a["mask_SxS2_ik0"]),
        "wq_s": a["L0_attn_Wq"], "wk_s": a["L0_attn_Wk"], "wv_s": a["L0_attn_Wv"], "wo_s": a["L0_attn_Wo"],
        "bq_s": a["L0_attn_bq"], "bk_s": a["L0_attn_bk"], "bv_s": a["L0_attn_bv"], "bo_s": a["L0_attn_bo"],
        "wq_x": a["L0_xattn_Wq"].T, "wk_x": a["L0_xattn_Wk"].T, "wv_x": a["L0_xattn_Wv"].T,
        "wo_x": a["L0_xattn_Wo"].T,
        "bq_x": a["L0_xattn_bq"], "bk_x": a["L0_xattn_bk"], "bv_x": a["L0_xattn_bv"], "bo_x": a["L0_xattn_bo"],
        "wr": a["L0_ffn_router_w"].T, "br": a["L0_ffn_router_b"],
        "we": a["L0_ffn_expert_w"].transpose(2, 0, 1).reshape(D, E * D), "be": a["L0_ffn_expert_b"],
        "countdown": np.arange(NP, 0, -1).astype(np.float32),
    }
    nc = bacc.Bacc("TRN2", target_bir_lowering=False, num_devices=1)
    arrays, t = {}, {}
    for name, v in laid.items():
        v = np.ascontiguousarray(v)
        arrays["in_" + name] = v
        t[name] = nc.dram_tensor("in_" + name, v.shape, mybir.dt.from_np(v.dtype), kind="ExternalInput").ap()
    out = nc.dram_tensor("out_0", (Q, D), F32, kind="ExternalOutput").ap()
    decoder_layer(nc, t, out)
    r = run_bass_kernel_spmd(nc, [arrays], core_ids=[0])
    return r.results[0]["out_0"].reshape(1, Q, D)
```
